# Optimizing a Trainium2 kernel written in Bass

```python
import numpy as np
import jax
import jax.numpy as jnp

def _softmax(x, axis=-1):
    return jax.nn.softmax(x, axis=axis)
def _gelu(x):
    return jax.nn.gelu(x, approximate=True)
def _silu(x):
    return jax.nn.silu(x)
def _sigmoid(x):
    return jax.nn.sigmoid(x)
def _layernorm(x, axis=-1, eps=1e-5):
    m = jnp.mean(x, axis=axis, keepdims=True)
    v = jnp.var(x, axis=axis, keepdims=True)
    return (x - m) / jnp.sqrt(v + eps)
def _scatter_add(tgt, idx, src, axis=0):
    return tgt.at[idx].add(src)
def _segment_sum(src, seg, n):
    return jax.ops.segment_sum(src, seg, n)

kernel_name = 'mk_conv_seq_d2_conv_nchw256_17440b'

def setup_inputs(seed: int = 0):
    np.random.seed(seed)
    _w = jnp.asarray
    def _rec_inputs():
        import jax
        import jax.numpy as jnp
        _gk = jax.random.key(seed)
        x = -0.0005207 + 1.001 * jax.random.normal(jax.random.fold_in(_gk, 1), (2, 256, 64, 64), jnp.float32)
        return x
    x = _rec_inputs()
    def _L0_conv_setup():
        import jax, jax.numpy as jnp
        import numpy as np
        B, C, H, W = (2, 256, 64, 64)
        NUM_HEADS = 8
        key = jax.random.key(seed)
        k1, k2, k3 = jax.random.split(key, 3)
        x = jax.random.normal(k1, (B, C, H, W), dtype=jnp.float32)
        w_qkv = jax.random.normal(k2, (3 * C, C), dtype=jnp.float32) * (1.0 / np.sqrt(C))
        w_proj = jax.random.normal(k3, (C, C), dtype=jnp.float32) * (1.0 / np.sqrt(C))
        return {'x': x, 'w_qkv': w_qkv, 'w_proj': w_proj}
    _L0_conv_all = _L0_conv_setup()
    _L0_conv_in = {k: v for k, v in _L0_conv_all.items() if k in ('w_qkv', 'w_proj', )}
    del _L0_conv_all

    def _L1_conv_setup():
        import jax, jax.numpy as jnp
        import numpy as np
        B, C, H, W = (8, 256, 64, 64)
        CM = C // 4
        CI = C - CM
        EPS = 1e-05

        def _conv1x1(t, w, b):
            return jnp.einsum('bchw,oc->bohw', t, w) + b[None, :, None, None]

        def _maxpool2(t):
            b, c, h, w = t.shape
            return t.reshape(b, c, h // 2, 2, w // 2, 2).max(axis=(3, 5))
        key = jax.random.key(seed)
        ks = jax.random.split(key, 12)
        return {'x': jax.random.normal(ks[0], (B, C, H, W), dtype=jnp.float32), 'g_w': jax.random.normal(ks[1], (C, C), dtype=jnp.float32) * 0.05, 'g_b': jax.random.normal(ks[2], (C,), dtype=jnp.float32) * 0.01, 'theta_w': jax.random.normal(ks[3], (CM, CM), dtype=jnp.float32) * 0.1, 'theta_b': jax.random.normal(ks[4], (CM,), dtype=jnp.float32) * 0.01, 'phi_w': jax.random.normal(ks[5], (CM, CI), dtype=jnp.float32) * 0.06, 'phi_b': jax.random.normal(ks[6], (CM,), dtype=jnp.float32) * 0.01, 'W_w': jax.random.normal(ks[7], (C, C), dtype=jnp.float32) * 0.05, 'W_b': jax.random.normal(ks[8], (C,), dtype=jnp.float32) * 0.01, 'bn_gamma': jax.random.normal(ks[9], (C,), dtype=jnp.float32) * 0.1 + 1.0, 'bn_beta': jax.random.normal(ks[10], (C,), dtype=jnp.float32) * 0.01, 'bn_mean': jax.random.normal(ks[11], (C,), dtype=jnp.float32) * 0.1, 'bn_var': jnp.ones((C,), dtype=jnp.float32)}
    _L1_conv_all = _L1_conv_setup()
    _L1_conv_in = {k: v for k, v in _L1_conv_all.items() if k in ('g_w', 'g_b', 'theta_w', 'theta_b', 'phi_w', 'phi_b', 'W_w', 'W_b', 'bn_gamma', 'bn_beta', 'bn_mean', 'bn_var', )}
    del _L1_conv_all

    return {
        "x": x,
        "L0_conv_w_qkv": _L0_conv_in["w_qkv"],
        "L0_conv_w_proj": _L0_conv_in["w_proj"],
        "L1_conv_g_w": _L1_conv_in["g_w"],
        "L1_conv_g_b": _L1_conv_in["g_b"],
        "L1_conv_theta_w": _L1_conv_in["theta_w"],
        "L1_conv_theta_b": _L1_conv_in["theta_b"],
        "L1_conv_phi_w": _L1_conv_in["phi_w"],
        "L1_conv_phi_b": _L1_conv_in["phi_b"],
        "L1_conv_W_w": _L1_conv_in["W_w"],
        "L1_conv_W_b": _L1_conv_in["W_b"],
        "L1_conv_bn_gamma": _L1_conv_in["bn_gamma"],
        "L1_conv_bn_beta": _L1_conv_in["bn_beta"],
        "L1_conv_bn_mean": _L1_conv_in["bn_mean"],
        "L1_conv_bn_var": _L1_conv_in["bn_var"],
    }

def reference(x, L0_conv_w_qkv, L0_conv_w_proj, L1_conv_g_w, L1_conv_g_b, L1_conv_theta_w, L1_conv_theta_b, L1_conv_phi_w, L1_conv_phi_b, L1_conv_W_w, L1_conv_W_b, L1_conv_bn_gamma, L1_conv_bn_beta, L1_conv_bn_mean, L1_conv_bn_var):
    import jax
    import jax.numpy as jnp
    def _L0_conv_ref(x, w_qkv, w_proj):
        import jax, jax.numpy as jnp
        import numpy as np
        B, C, H, W = (2, 256, 64, 64)
        NUM_HEADS = 8
        b, c, h, w = x.shape
        hd = NUM_HEADS
        d = c // hd
        n = h * w
        qkv = jnp.einsum('oc,bchw->bohw', w_qkv, x)
        q, k, v = jnp.split(qkv, 3, axis=1)

        def reshape(t):
            return t.reshape(b, hd, d, n)
        q, k, v = map(reshape, (q, k, v))
        scores = jnp.einsum('bhdi,bhdj->bhij', q, k) / jnp.sqrt(jnp.asarray(d, x.dtype))
        attn = jax.nn.softmax(scores, axis=-1)
        out = jnp.einsum('bhij,bhdj->bhdi', attn, v)
        out = out.reshape(b, c, h, w)
        return jnp.einsum('oc,bchw->bohw', w_proj, out) + x

    def _L1_conv_ref(x, g_w, g_b, theta_w, theta_b, phi_w, phi_b, W_w, W_b, bn_gamma, bn_beta, bn_mean, bn_var):
        import jax, jax.numpy as jnp
        import numpy as np
        B, C, H, W = (8, 256, 64, 64)
        CM = C // 4
        CI = C - CM
        EPS = 1e-05

        def _conv1x1(t, w, b):
            return jnp.einsum('bchw,oc->bohw', t, w) + b[None, :, None, None]

        def _maxpool2(t):
            b, c, h, w = t.shape
            return t.reshape(b, c, h // 2, 2, w // 2, 2).max(axis=(3, 5))
        b, c, h, w = x.shape
        ci = c // 4
        mask_ch = x[:, :ci]
        img_ch = x[:, ci:]
        g_x = _maxpool2(_conv1x1(x, g_w, g_b)).reshape(b, c, -1).transpose(0, 2, 1)
        theta_x = _conv1x1(mask_ch, theta_w, theta_b).reshape(b, ci, -1).transpose(0, 2, 1)
        phi_x = _maxpool2(_conv1x1(img_ch, phi_w, phi_b)).reshape(b, ci, -1)
        f = jnp.einsum('bnc,bcm->bnm', theta_x, phi_x)
        f_div_C = jax.nn.softmax(f, axis=-1)
        y = jnp.einsum('bnm,bmc->bnc', f_div_C, g_x)
        y = y.transpose(0, 2, 1).reshape(b, c, h, w)
        W_y = _conv1x1(y, W_w, W_b)
        inv = jax.lax.rsqrt(bn_var + EPS)
        W_y = (W_y - bn_mean[None, :, None, None]) * (inv * bn_gamma)[None, :, None, None] + bn_beta[None, :, None, None]
        return W_y + x

    def _gn(v, G=32, eps=1e-5):
        B_, C_, H_, W_ = v.shape
        g = v.reshape(B_, G, C_ // G, H_, W_)
        m = jnp.mean(g, axis=(2, 3, 4), keepdims=True)
        s = jnp.var(g, axis=(2, 3, 4), keepdims=True)
        return ((g - m) / jnp.sqrt(s + eps)).reshape(v.shape)

    def _ln_c(v, eps=1e-6):
        m = jnp.mean(v, axis=1, keepdims=True)
        s = jnp.var(v, axis=1, keepdims=True)
        return (v - m) / jnp.sqrt(s + eps)

    def _ln_t(v, eps=1e-5):
        m = jnp.mean(v, axis=-1, keepdims=True)
        s = jnp.var(v, axis=-1, keepdims=True)
        return (v - m) / jnp.sqrt(s + eps)

    def _to_tokens(v):
        B_, C_, H_, W_ = v.shape
        return v.reshape(B_, C_, H_ * W_).transpose(0, 2, 1)
    def _from_tokens(t, like):
        B_, C_, H_, W_ = like.shape
        return t.transpose(0, 2, 1).reshape(B_, C_, H_, W_)

    x = _L0_conv_ref(x, L0_conv_w_qkv, L0_conv_w_proj)
    x = _L1_conv_ref(x, L1_conv_g_w, L1_conv_g_b, L1_conv_theta_w, L1_conv_theta_b, L1_conv_phi_w, L1_conv_phi_b, L1_conv_W_w, L1_conv_W_b, L1_conv_bn_gamma, L1_conv_bn_beta, L1_conv_bn_mean, L1_conv_bn_var)
    return x


_drawn_inputs = setup_inputs


def setup_inputs(seed=0):
    import zlib

    import numpy as np

    out = dict(_drawn_inputs(seed))
    spreads = {'L1_conv_bn_var': (1.0, 0.2)}
    factors = {'L1_conv_g_b': 8.0,
     'L1_conv_theta_b': 8.0,
     'L1_conv_phi_b': 8.0,
     'L1_conv_W_b': 7.242,
     'L1_conv_bn_beta': 6.689}
    for name, (base, spread) in spreads.items():
        noise = np.random.default_rng([zlib.crc32(name.encode()), seed]).standard_normal(out[name].shape)
        drawn = base * np.exp(spread * noise) if base else spread * noise
        out[name] = jnp.asarray(drawn.astype(out[name].dtype))
    for name, factor in factors.items():
        out[name] = (out[name] * factor).astype(out[name].dtype)
    return out
```

```python
from contextlib import ExitStack

import concourse.bass as bass
from concourse import mybir

ALU = mybir.AluOpType
ACT = mybir.ActivationFunctionType
AX = mybir.AxisListType
F32 = mybir.dt.float32
F16 = mybir.dt.float16

B, C, H, W = 2, 256, 64, 64
N = H * W
CT = C // 128
HEADS, D = 8, 32
G = 4
NG = HEADS // G
CH = 512
NC = N // CH
JT = N // 128
CM = C // 4
M = N // 4
MT = M // 128
EPS = 1e-5

QS = 16.0
MW = 1024.0
SCORE = 1.0 / (QS * QS * float(D) ** 0.5)

RING = 4
SIZES = [3, 3, 2, 3, 3, 2] * 8
NOPS = len(SIZES)
UNITS = JT * G
STARTS = [sum(SIZES[:o]) for o in range(NOPS)]
SUM_PE = [5, 12, 19, 29, 30, 31]
SUM_V = [j for j in range(JT) if j not in SUM_PE]


def adds_through(j):
    return max(1, sum(1 for t in SUM_V if t <= j) - 1)


ADDS = adds_through(JT - 1)
DONE_BY = [next(o for o in range(NOPS) if STARTS[o] + SIZES[o] >= G * (j + 1)) for j in range(JT)]
assert sum(SIZES) == UNITS and SUM_V[:2] == [0, 1]


def conv_seq(nc, x, wqkv, wproj, gw, gb, tw, tb, pw, pb, ww, wb, bn_g, bn_b, bn_m, bn_v, out, o_dram, l_dram, r_dram):
    x_v = x.rearrange("b (t p) n -> b p t n", p=128)
    out_v = out.rearrange("b (t p) n -> b p t n", p=128)
    o_v = o_dram.rearrange("b (t p) n -> b p t n", p=128)

    with ExitStack() as root:
        used = {}

        def unique(name):
            used[name] = used.get(name, 0) + 1
            return name if used[name] == 1 else f"{name}_{used[name]}"

        def sb(ctx, name, shape, dt=F32):
            return ctx.enter_context(nc.sbuf_tensor(unique(name), shape, dt))

        def sem(ctx, name):
            return ctx.enter_context(nc.semaphore(unique(name)))

        bank = [root.enter_context(nc.psum_tensor(f"bank{i}", [128, 1536], F32)) for i in range(2)]
        psOL = root.enter_context(nc.psum_tensor("psOL", [128, 2 * CH], F32))
        psO, psL = psOL[:, 0:CH], psOL[:, CH:2 * CH]

        def slot(i):
            return bank[i % 6 // 3][:, (i % 3) * CH:(i % 3 + 1) * CH]

        wq_sb = sb(root, "wq_sb", [128, CT, 3 * C])
        wp_sb = sb(root, "wp_sb", [128, CT, C])
        gw_sb = sb(root, "gw_sb", [128, CT, C])
        ww_sb = sb(root, "ww_sb", [128, CT, C])
        tw_sb = sb(root, "tw_sb", [128, CM])
        pw_sb = sb(root, "pw_sb", [128, CT, CM])
        col = sb(root, "col", [128, CT, 8])
        tb_sb = sb(root, "tb_sb", [CM, 2])
        sA = sb(root, "sA", [128, CT, 3])
        epsc = sb(root, "epsc", [128, 1])
        ident = sb(root, "ident", [128, 128])
        ones = sb(root, "ones", [128, 128])
        X = sb(root, "X", [128, CT, N])

        def end_phase(ctx, sems):
            with nc.Block() as block:
                @block.gpsimd
                def _(pool):
                    for s in sems:
                        pool.sem_clear(s)

        with ExitStack() as ctx:
            s_w = sem(ctx, "s_w")
            s_zero = sem(ctx, "s_zero")
            s_id = sem(ctx, "s_id")
            s_sq = sem(ctx, "s_sq")
            s_bn = sem(ctx, "s_bn")
            loads = [(wq_sb[:], wqkv.rearrange("(t p) o -> p t o", p=128)),
                     (wp_sb[:], wproj.rearrange("(t p) o -> p t o", p=128)),
                     (gw_sb[:], gw.rearrange("(t p) o -> p t o", p=128)),
                     (ww_sb[:], ww.rearrange("(t p) o -> p t o", p=128))]
            small = [(tw_sb[0:CM, :], tw), (pw_sb[CM:128, 0, :], pw[0:128 - CM, :]),
                     (pw_sb[:, 1, :], pw[128 - CM:, :]),
                     (tb_sb[:, 0:1], tb.rearrange("(p a) -> p a", a=1)),
                     (tb_sb[:, 1:2], pb.rearrange("(p a) -> p a", a=1))]
            for k, v in enumerate((gb, wb, bn_g, bn_b, bn_m, bn_v)):
                for t in range(CT):
                    small.append((col[:, t, k:k + 1], v[t * 128:(t + 1) * 128].rearrange("(p a) -> p a", a=1)))
            with nc.Block() as block:
                @block.sync
                def _(sp):
                    for dst, src in loads:
                        sp.dma_start(dst, src).then_inc(s_w, 16)
                    sp.wait_ge(s_zero, 2)
                    for dst, src in small:
                        sp.dma_start(dst, src).then_inc(s_w, 16)
                    sp.wait_ge(s_w, 16 * (len(loads) + len(small)))

                @block.gpsimd
                def _(pool):
                    nc.gpsimd.memset(ident[:], 0.0).then_inc(s_id, 1)
                    pool.wait_ge(s_id, 1)
                    nc.gpsimd.affine_select(out=ident[:], in_=ident[:], compare_op=ALU.not_equal, fill=1.0,
                                            base=0, pattern=[[-1, 128]], channel_multiplier=1).then_inc(s_id, 1)
                    pool.wait_ge(s_id, 2)

                @block.vector
                def _(dve):
                    nc.vector.memset(tw_sb[:], 0.0).then_inc(s_zero, 1)
                    nc.vector.memset(pw_sb[:, 0, :], 0.0).then_inc(s_zero, 1)
                    nc.vector.memset(ones[:], 1.0)
                    dve.wait_ge(s_w, 16 * (len(loads) + len(small)))
                    nc.vector.tensor_scalar(sA[:, :, 0], col[:, :, 5], EPS, None, ALU.add).then_inc(s_bn, 1)
                    dve.wait_ge(s_bn, 1)
                    nc.vector.reciprocal(sA[:, :, 1], sA[:, :, 0]).then_inc(s_bn, 1)
                    dve.wait_ge(s_sq, 1)
                    nc.vector.tensor_tensor(sA[:, :, 1], sA[:, :, 0], col[:, :, 2], ALU.mult).then_inc(s_bn, 1)
                    nc.vector.tensor_tensor(col[:, :, 6], col[:, :, 1], col[:, :, 4], ALU.subtract).then_inc(s_bn, 1)
                    dve.wait_ge(s_bn, 4)
                    nc.vector.tensor_tensor(col[:, :, 7], col[:, :, 6], sA[:, :, 1], ALU.mult).then_inc(s_bn, 1)
                    dve.wait_ge(s_bn, 5)
                    nc.vector.tensor_tensor(sA[:, :, 2], col[:, :, 7], col[:, :, 3], ALU.add).then_inc(s_bn, 1)
                    dve.wait_ge(s_bn, 6)

                @block.scalar
                def _(act):
                    act.wait_ge(s_bn, 2)
                    nc.scalar.activation(sA[:, :, 0], sA[:, :, 1], ACT.Sqrt).then_inc(s_sq, 1)
            end_phase(ctx, [s_w, s_zero, s_id, s_sq, s_bn])

        def layer0(b):
            with ExitStack() as ctx:
                Qst = sb(ctx, "Qst", [128, G, N], F16)
                Kst = sb(ctx, "Kst", [128, G, N], F16)
                V = sb(ctx, "V", [128, JT, C])
                s_x = sem(ctx, "s_x")
                s_pad = sem(ctx, "s_pad")
                s_mm = sem(ctx, "s_mm")
                s_ev = sem(ctx, "s_ev")
                s_hi = sem(ctx, "s_hi")
                with nc.Block() as block:
                    @block.sync
                    def _(sp):
                        for t in range(CT):
                            sp.dma_start(X[:, t, :], x_v[b, :, t, :]).then_inc(s_x, 16)

                    @block.gpsimd
                    def _(pool):
                        nc.gpsimd.memset(Qst[96:128, :, :], 0.0)
                        nc.gpsimd.memset(Kst[96:128, :, :], 0.0).then_inc(s_pad, 1)
                        pool.wait_ge(s_pad, 1)
                        nc.gpsimd.memset(Kst[96:97, :, :], MW).then_inc(s_pad, 1)
                        pool.wait_ge(s_pad, 2)

                    @block.tensor
                    def _(pe):
                        pe.wait_ge(s_x, 16 * CT)
                        for j in range(JT):
                            if j >= 6:
                                pe.wait_ge(s_ev, j - 5)
                            for t in range(CT):
                                last = nc.tensor.matmul(slot(j)[:, 0:C], X[:, t, j * 128:(j + 1) * 128],
                                                        wq_sb[:, t, 2 * C:3 * C], start=(t == 0), stop=(t == CT - 1))
                            last.then_inc(s_mm, 1)

                    @block.vector
                    def _(dve):
                        for j in range(JT):
                            dve.wait_ge(s_mm, j + 1)
                            nc.vector.tensor_copy(V[:, j, :], slot(j)[:, 0:C]).then_inc(s_ev, 1)
                        dve.wait_ge(s_ev, JT)
                end_phase(ctx, [s_x, s_pad, s_mm, s_ev])

                for g in range(NG):
                    with ExitStack() as c2:
                        hi = [sb(c2, f"hi{k}", [128, N], F16) for k in range(2)]
                        lo = [sb(c2, f"lo{k}", [128, N], F16) for k in range(2)]
                        s_st = sem(c2, "s_st")
                        with nc.Block() as block:
                            @block.tensor
                            def _(pe):
                                for u in range(2 * NC):
                                    k, c = divmod(u, NC)
                                    if u >= 6:
                                        pe.wait_ge(s_ev, u - 5)
                                    for t in range(CT):
                                        w = wq_sb[:, t, k * C + g * 128:k * C + (g + 1) * 128]
                                        last = nc.tensor.matmul(slot(u), w, X[:, t, c * CH:(c + 1) * CH],
                                                                start=(t == 0), stop=(t == CT - 1))
                                    last.then_inc(s_mm, 1)

                            @block.scalar
                            def _(act):
                                for u in range(2 * NC):
                                    k, c = divmod(u, NC)
                                    act.wait_ge(s_mm, u + 1)
                                    nc.scalar.activation(hi[k][:, c * CH:(c + 1) * CH], slot(u), ACT.Copy,
                                                         scale=QS).then_inc(s_hi, 1)

                            @block.vector
                            def _(dve):
                                for u in range(2 * NC):
                                    k, c = divmod(u, NC)
                                    dve.wait_ge(s_hi, u + 1)
                                    nc.vector.scalar_tensor_tensor(
                                        out=lo[k][:, c * CH:(c + 1) * CH], in0=slot(u), scalar=QS,
                                        in1=hi[k][:, c * CH:(c + 1) * CH],
                                        op0=ALU.mult, op1=ALU.subtract).then_inc(s_ev, 1)

                            @block.sync
                            def _(sp):
                                n = 0
                                for k, dst, parts in ((0, Qst, (hi[0], lo[0], hi[0])), (1, Kst, (hi[1], hi[1], lo[1]))):
                                    sp.wait_ge(s_ev, NC * (k + 1))
                                    for h in range(G):
                                        for r, part in enumerate(parts):
                                            sp.dma_start(dst[r * D:(r + 1) * D, h, :],
                                                         part[h * D:(h + 1) * D, :]).then_inc(s_st, 16)
                                            n += 16
                                sp.wait_ge(s_st, n)
                        end_phase(c2, [s_mm, s_ev, s_hi, s_st])

                    with ExitStack() as c2:
                        mp = sb(c2, "mp", [128, G, JT, 3])
                        mcol = sb(c2, "mcol", [128, G * JT])
                        mrow = sb(c2, "mrow", [128, 128], F16)
                        s_s = sem(c2, "s_s")
                        s_m = sem(c2, "s_m")
                        s_t = sem(c2, "s_t")
                        s_r = sem(c2, "s_r")
                        parts = [(0, 3), (3, 6), (6, 8)]
                        n_it = G * len(parts)
                        with nc.Block() as block:
                            @block.tensor
                            def _(pe):
                                with pe.Fori(0, JT) as it:
                                    for h in range(G):
                                        for k, (c0, c1) in enumerate(parts):
                                            o = h * 3 + k
                                            pe.wait_ge(s_m, it * n_it + o + 1)
                                            for c in range(c0, c1):
                                                last = nc.tensor.matmul(
                                                    bank[o % 2][:, (c - c0) * CH:(c - c0 + 1) * CH],
                                                    Qst[0:96, h, bass.ds(it * 128, 128)],
                                                    Kst[0:96, h, c * CH:(c + 1) * CH], start=True, stop=True)
                                            last.then_inc(s_s, 1)
                                pe.wait_ge(s_t, 1)
                                nc.tensor.transpose(psL[:, 0:128], mcol[:, :], ident[:, :]).then_inc(s_s, 1)

                            @block.vector
                            def _(dve):
                                dve.sem_inc(s_m, 2)
                                with dve.Fori(0, JT) as it:
                                    for h in range(G):
                                        for k, (c0, c1) in enumerate(parts):
                                            o = h * 3 + k
                                            dve.wait_ge(s_s, it * n_it + o + 1)
                                            nc.vector.tensor_reduce(
                                                mp[:, h, bass.ds(it, 1), k], bank[o % 2][:, 0:(c1 - c0) * CH],
                                                AX.X, ALU.max).then_inc(s_m, 1)
                                dve.wait_ge(s_m, 2 + JT * n_it)
                                nc.vector.tensor_reduce(mcol[:, :], mp[:].rearrange("p h i k -> p (h i) k"),
                                                        AX.X, ALU.max).then_inc(s_t, 1)
                                dve.wait_ge(s_s, JT * n_it + 1)
                                nc.vector.tensor_scalar(mrow[:, :], psL[:, 0:128], -1.0 / MW, None,
                                                        ALU.mult).then_inc(s_t, 1)

                            @block.sync
                            def _(sp):
                                sp.wait_ge(s_t, 2)
                                for h in range(G):
                                    sp.dma_start(Qst[96:97, h, :], mrow[h * JT:(h + 1) * JT, :]).then_inc(s_r, 16)
                                sp.wait_ge(s_r, 16 * G)
                        end_phase(c2, [s_s, s_m, s_t, s_r])

                    with ExitStack() as c2:
                        P = sb(c2, "P", [128, RING * G, CH])
                        acc = sb(c2, "acc", [128, G, CH])
                        OL = sb(c2, "OL", [128, 2 * CH])
                        s_ready = sem(c2, "s_ready")
                        s_exp = sem(c2, "s_exp")
                        s_pv = sem(c2, "s_pv")
                        s_add = sem(c2, "s_add")
                        s_accr = sem(c2, "s_accr")
                        s_o = sem(c2, "s_o")
                        s_free = sem(c2, "s_free")
                        s_out = sem(c2, "s_out")

                        with nc.Block() as block:
                            @block.tensor
                            def _(pe):
                                def scores(before, o, c):
                                    if before is not None:
                                        pe.wait_ge(s_exp, before)
                                    for k in range(SIZES[o]):
                                        j, h = divmod(STARTS[o] + k, G)
                                        last = nc.tensor.matmul(bank[o % 2][:, k * CH:(k + 1) * CH],
                                                                Kst[:, h, j * 128:(j + 1) * 128],
                                                                Qst[:, h, bass.ds(c * CH, CH)], start=True, stop=True)
                                    last.then_inc(s_ready, 1)

                                def sums(src, first, last):
                                    for h in range(G):
                                        mm = nc.tensor.matmul(psL[h * D:(h + 1) * D, :], ones[:, 0:D], src(h),
                                                              start=first, stop=last)
                                    return mm

                                def values(c, j):
                                    pe.wait_ge(s_exp, c * NOPS + DONE_BY[j] + 1)
                                    if j == 0:
                                        pe.wait_ge(s_free, c + 1)
                                    for h in range(G):
                                        last = nc.tensor.matmul(psO[h * D:(h + 1) * D, :],
                                                                V[:, j, g * 128 + h * D:g * 128 + (h + 1) * D],
                                                                P[:, (j % RING) * G + h, :],
                                                                start=(j == 0), stop=(j == JT - 1))
                                    if j in SUM_PE:
                                        last = sums(lambda h: P[:, (j % RING) * G + h, :], j == SUM_PE[0], j == JT - 1)
                                    last.then_inc(s_pv, 1)
                                    if j == JT - 2:
                                        pe.wait_ge(s_add, (c + 2) * ADDS)
                                        sums(lambda h: acc[:, h, :], False, False).then_inc(s_accr, 1)

                                def chunk(c, go_on):
                                    nxt = 0
                                    for o in range(NOPS):
                                        if o + 2 < NOPS:
                                            scores(c * NOPS + o + 1, o + 2, c)
                                        elif go_on:
                                            scores(c * NOPS + o + 1, o + 2 - NOPS, c + 1)
                                        while nxt < JT and DONE_BY[nxt] <= o:
                                            values(c, nxt)
                                            nxt += 1

                                for o in range(2):
                                    scores(None, o, 0)
                                with pe.Fori(0, NC - 1) as c:
                                    chunk(c, True)
                                chunk(NC - 1, False)

                            @block.scalar
                            def _(act):
                                with act.Fori(0, NC) as c:
                                    for o in range(NOPS):
                                        act.wait_ge(s_ready, c * NOPS + o + 1)
                                        u0 = STARTS[o]
                                        j0, j1 = u0 // G, (u0 + SIZES[o] - 1) // G
                                        if j0 != j1 or u0 % G == 0:
                                            act.wait_ge(s_pv, c * JT + j1 + 1)
                                            if j1 >= RING:
                                                act.wait_ge(s_add, (c + 1) * ADDS + adds_through(j1 - RING))
                                            else:
                                                act.wait_ge(s_add, c * ADDS + adds_through(j1 - RING + JT))
                                        r = u0 % (RING * G)
                                        s3 = bank[o % 2][:, 0:SIZES[o] * CH].rearrange("p (u n) -> p u n", n=CH)
                                        nc.scalar.activation(P[:, r:r + SIZES[o], :], s3, ACT.Exp,
                                                             scale=SCORE).then_inc(s_exp, 1)

                            @block.vector
                            def _(dve):
                                dve.sem_inc(s_pv, RING)
                                dve.sem_inc(s_add, ADDS)
                                dve.sem_inc(s_accr, 1)
                                dve.sem_inc(s_free, 1)
                                dve.sem_inc(s_out, 32)
                                with dve.Fori(0, NC) as c:
                                    for n, j in enumerate(SUM_V[1:]):
                                        dve.wait_ge(s_exp, c * NOPS + DONE_BY[j] + 1)
                                        new = P[:, (j % RING) * G:(j % RING + 1) * G, :]
                                        if n == 0:
                                            dve.wait_ge(s_accr, c + 1)
                                            old = P[:, 0:G, :]
                                        else:
                                            dve.wait_ge(s_add, (c + 1) * ADDS + n)
                                            old = acc[:]
                                        nc.vector.tensor_tensor(acc[:], old, new, ALU.add).then_inc(s_add, 1)
                                    dve.wait_ge(s_pv, RING + (c + 1) * JT)
                                    dve.wait_ge(s_out, 32 * (c + 1))
                                    nc.vector.tensor_copy(OL[:], psOL[:]).then_inc(s_free, 1)

                            @block.sync
                            def _(sp):
                                with sp.Fori(0, NC) as c:
                                    sp.wait_ge(s_free, c + 2)
                                    sp.dma_start(o_dram[b, g * 128:(g + 1) * 128, bass.ds(c * CH, CH)],
                                                 OL[:, 0:CH]).then_inc(s_out, 16)
                                    sp.dma_start(l_dram[b, g * G:(g + 1) * G, bass.ds(c * CH, CH)],
                                                 OL[0:128:D, CH:2 * CH]).then_inc(s_out, 16)
                                sp.wait_ge(s_out, 32 * (NC + 1))
                        end_phase(c2, [s_ready, s_exp, s_pv, s_add, s_accr, s_free, s_out])

        def layer1(b):
            with ExitStack() as ctx:
                O = sb(ctx, "O", [128, CT, N])
                T = sb(ctx, "T", [128, N])
                s_in = sem(ctx, "s_in")
                s_rec = sem(ctx, "s_rec")
                s_mm = sem(ctx, "s_mm1")
                s_ev = sem(ctx, "s_ev1")
                with ExitStack() as c2:
                    R = sb(c2, "R", [128, CT, N])
                    L = sb(c2, "L", [128, HEADS * N // 128])
                    Li = sb(c2, "Li", [128, HEADS * N // 128])
                    s_l = sem(c2, "s_l")
                    s_norm = sem(c2, "s_norm")
                    with nc.Block() as block:
                        @block.sync
                        def _(sp):
                            sp.dma_start(L[:], l_dram[b].rearrange("h (a n) -> (h a) n", n=HEADS * N // 128)
                                         ).then_inc(s_l, 16)
                            for t in range(CT):
                                sp.dma_start(O[:, t, :], o_v[b, :, t, :]).then_inc(s_in, 16)
                            sp.wait_ge(s_rec, 1)
                            sp.dma_start(r_dram[b].rearrange("h (a n) -> (h a) n", n=HEADS * N // 128),
                                         Li[:]).then_inc(s_l, 16)
                            sp.wait_ge(s_l, 32)
                            for h in range(HEADS):
                                sp.dma_start(R[h % G * D:(h % G + 1) * D, h // G, :],
                                             r_dram[b, h:h + 1, :].broadcast_to([D, N])).then_inc(s_in, 16)

                        @block.vector
                        def _(dve):
                            dve.wait_ge(s_l, 16)
                            nc.vector.reciprocal(Li[:], L[:]).then_inc(s_rec, 1)
                            dve.wait_ge(s_in, 16 * (CT + HEADS))
                            for c in range(NC):
                                cs = slice(c * CH, (c + 1) * CH)
                                nc.vector.tensor_tensor(O[:, :, cs], O[:, :, cs], R[:, :, cs], ALU.mult
                                                        ).then_inc(s_norm, 1)
                            for u in range(NC * CT):
                                c, t = divmod(u, CT)
                                cs = slice(c * CH, (c + 1) * CH)
                                dve.wait_ge(s_mm, u + 1)
                                nc.vector.tensor_tensor(X[:, t, cs], X[:, t, cs], slot(u), ALU.add
                                                        ).then_inc(s_ev, 1)
                            dve.wait_ge(s_ev, NC * CT)

                        @block.tensor
                        def _(pe):
                            for u in range(NC * CT):
                                c, t = divmod(u, CT)
                                pe.wait_ge(s_norm, c + 1)
                                if u >= 6:
                                    pe.wait_ge(s_ev, u - 5)
                                for k in range(CT):
                                    last = nc.tensor.matmul(slot(u), wp_sb[:, k, t * 128:(t + 1) * 128],
                                                            O[:, k, c * CH:(c + 1) * CH],
                                                            start=(k == 0), stop=(k == CT - 1))
                                last.then_inc(s_mm, 1)
                    end_phase(c2, [s_in, s_rec, s_mm, s_ev, s_l, s_norm])

                Ph = sb(ctx, "Ph", [128, M])
                GT = sb(ctx, "GT", [128, MT, C])
                s_pad = sem(ctx, "s_pad1")
                with ExitStack() as c2:
                    Gp = sb(c2, "Gp", [128, CT, M])
                    pooled = sb(c2, "pooled", [128, 2, CH // 4])
                    s_pool = sem(c2, "s_pool")
                    UN = 4
                    with nc.Block() as block:
                        @block.gpsimd
                        def _(pool):
                            nc.gpsimd.memset(T[CM:128, :], 0.0)
                            nc.gpsimd.memset(Ph[CM:128, :], 0.0).then_inc(s_pad, 1)
                            pool.wait_ge(s_pad, 1)
                            nc.gpsimd.memset(Ph[CM:CM + 1, :], 1.0).then_inc(s_pad, 1)
                            pool.wait_ge(s_pad, 2)

                        @block.tensor
                        def _(pe):
                            for u in range(UN * NC):
                                c, k = divmod(u, UN)
                                cs = slice(c * CH, (c + 1) * CH)
                                if u >= 6:
                                    pe.wait_ge(s_ev, u - 5)
                                if k == 0:
                                    last = nc.tensor.matmul(slot(u)[0:CM, :], tw_sb[:], X[:, 0, cs], start=True, stop=True)
                                else:
                                    for t in range(CT):
                                        w = pw_sb[:, t, :] if k == 1 else gw_sb[:, t, (k - 2) * 128:(k - 1) * 128]
                                        last = nc.tensor.matmul(slot(u)[0:CM if k == 1 else 128, :], w, X[:, t, cs],
                                                                start=(t == 0), stop=(t == CT - 1))
                                last.then_inc(s_mm, 1)
                            pe.wait_ge(s_ev, UN * NC)
                            for m in range(MT):
                                if m >= 6:
                                    pe.wait_ge(s_ev, UN * NC + m - 5)
                                for t in range(CT):
                                    last = nc.tensor.matmul(slot(m)[:, 0:C], Gp[:, t, m * 128:(m + 1) * 128],
                                                            ww_sb[:, t, :], start=(t == 0), stop=(t == CT - 1))
                                last.then_inc(s_mm, 1)

                        @block.vector
                        def _(dve):
                            pools = 0
                            for u in range(UN * NC):
                                c, k = divmod(u, UN)
                                dve.wait_ge(s_mm, u + 1)
                                if k == 0:
                                    nc.vector.tensor_scalar(T[0:CM, c * CH:(c + 1) * CH], slot(u)[0:CM, :],
                                                            tb_sb[:, 0:1], None, ALU.add).then_inc(s_ev, 1)
                                    continue
                                P0 = CM if k == 1 else 128
                                q = CH // 4
                                tmp = pooled[0:P0, pools % 2, :]
                                src = slot(u)[0:P0, :].rearrange("p (a u b v) -> p a b u v", u=2, v=2, b=W // 2)
                                nc.vector.tensor_reduce(tmp.rearrange("p (a b) -> p a b", b=W // 2), src, AX.XY,
                                                        ALU.max).then_inc(s_pool, 1)
                                pools += 1
                                dve.wait_ge(s_pool, pools)
                                dst = Ph[0:CM, c * q:(c + 1) * q] if k == 1 else Gp[:, k - 2, c * q:(c + 1) * q]
                                bias = tb_sb[:, 1:2] if k == 1 else col[:, k - 2, 0:1]
                                nc.vector.tensor_scalar(dst, tmp, bias, None, ALU.add).then_inc(s_ev, 1)
                            for m in range(MT):
                                dve.wait_ge(s_mm, UN * NC + m + 1)
                                nc.vector.tensor_copy(GT[:, m, :], slot(m)[:, 0:C]).then_inc(s_ev, 1)
                            dve.wait_ge(s_ev, UN * NC + MT)
                    end_phase(c2, [s_pad, s_pool, s_mm, s_ev])

                R1 = sb(ctx, "R1", [128, N])
                with ExitStack() as c2:
                    stat = sb(c2, "stat", [128, 2, JT])
                    mx = sb(c2, "mx", [128, JT])
                    l1 = sb(c2, "l1", [128, JT])
                    junk = sb(c2, "junk", [128, M])
                    statT = sb(c2, "statT", [2 * JT, 128])
                    s_e = sem(c2, "s_e")
                    s_n = sem(c2, "s_n")
                    s_row = sem(c2, "s_row")
                    with nc.Block() as block:
                        @block.tensor
                        def _(pe):
                            for i in range(JT):
                                if i >= 2:
                                    pe.wait_ge(s_e, i - 1)
                                for k in range(M // CH):
                                    last = nc.tensor.matmul(bank[i % 2][:, k * CH:(k + 1) * CH],
                                                            T[:, i * 128:(i + 1) * 128],
                                                            Ph[:, k * CH:(k + 1) * CH], start=True, stop=True)
                                last.then_inc(s_mm, 1)
                            pe.wait_ge(s_n, JT + 1)
                            nc.tensor.transpose(psL[0:2 * JT, 0:128], stat[:].rearrange("p k i -> p (k i)"),
                                                ident[:, :]).then_inc(s_mm, 1)

                        @block.vector
                        def _(dve):
                            for i in range(JT):
                                dve.wait_ge(s_mm, i + 1)
                                nc.vector.tensor_reduce(mx[:, i:i + 1], bank[i % 2][:, 0:M], AX.X, ALU.max
                                                        ).then_inc(s_ev, 1)
                                dve.wait_ge(s_ev, i + 1)
                                nc.vector.tensor_scalar(stat[:, 0, i:i + 1], mx[:, i:i + 1], -1.0, None, ALU.mult
                                                        ).then_inc(s_n, 1)
                            dve.wait_ge(s_e, JT)
                            nc.vector.reciprocal(stat[:, 1, :], l1[:]).then_inc(s_n, 1)
                            dve.wait_ge(s_mm, JT + 1)
                            nc.vector.tensor_copy(statT[:], psL[0:2 * JT, 0:128]).then_inc(s_n, 1)

                        @block.scalar
                        def _(act):
                            for i in range(JT):
                                act.wait_ge(s_n, i + 1)
                                if i:
                                    act.wait_ge(s_e, i)
                                nc.scalar.activation(junk[:], bank[i % 2][:, 0:M], ACT.Exp, bias=stat[:, 0, i:i + 1],
                                                     accum_out=l1[:, i:i + 1]).then_inc(s_e, 1)

                        @block.sync
                        def _(sp):
                            sp.wait_ge(s_n, JT + 2)
                            sp.dma_start(T[CM:CM + 1, :], statT[0:JT, :]).then_inc(s_row, 16)
                            sp.dma_start(r_dram[b, 0:1, :].rearrange("a (i n) -> (a i) n", n=128),
                                         statT[JT:2 * JT, :]).then_inc(s_row, 16)
                            sp.wait_ge(s_row, 32)
                            sp.dma_start(R1[:], r_dram[b, 0:1, :].broadcast_to([128, N])).then_inc(s_row, 16)
                            sp.wait_ge(s_row, 48)
                    end_phase(c2, [s_mm, s_ev, s_e, s_n, s_row])

                with ExitStack() as c2:
                    PT = sb(c2, "PT", [128, 2, MT, CH])
                    z = sb(c2, "z", [128, 2, CH])
                    res = sb(c2, "res", [128, 2, CH])
                    s_s = sem(c2, "s_s1")
                    s_e = sem(c2, "s_e1")
                    s_y = sem(c2, "s_y")
                    s_yf = sem(c2, "s_yf")
                    s_z = sem(c2, "s_z")
                    s_res = sem(c2, "s_res")
                    s_st = sem(c2, "s_st1")
                    SZ = [3, 3, 2]
                    with nc.Block() as block:
                        @block.tensor
                        def _(pe):
                            with pe.Fori(0, NC // 2) as i:
                                for p in range(2):
                                    for k in range(3):
                                        o = 3 * p + k
                                        pe.wait_ge(s_e, i * 6 + o + 1)
                                        for r in range(SZ[k]):
                                            m = 3 * k + r
                                            last = nc.tensor.matmul(bank[o % 2][:, r * CH:(r + 1) * CH],
                                                                    Ph[:, m * 128:(m + 1) * 128],
                                                                    T[:, bass.ds(i * 2 * CH + p * CH, CH)],
                                                                    start=True, stop=True)
                                        last.then_inc(s_s, 1)
                                for p in range(2):
                                    pe.wait_ge(s_e, i * 6 + 3 * p + 5)
                                    for t in range(CT):
                                        pe.wait_ge(s_yf, i * 4 + 2 * p + t + 1)
                                        for m in range(MT):
                                            last = nc.tensor.matmul(psOL[:, t * CH:(t + 1) * CH],
                                                                    GT[:, m, t * 128:(t + 1) * 128],
                                                                    PT[:, p, m, :], start=(m == 0), stop=(m == MT - 1))
                                        last.then_inc(s_y, 1)

                        @block.scalar
                        def _(act):
                            with act.Fori(0, NC // 2) as i:
                                for p in range(2):
                                    act.wait_ge(s_y, i * 4 + 2 * p + 2)
                                    for k in range(3):
                                        o = 3 * p + k
                                        act.wait_ge(s_s, i * 6 + o + 1)
                                        nc.scalar.activation(
                                            PT[:, p, 3 * k:3 * k + SZ[k], :],
                                            bank[o % 2][:, 0:SZ[k] * CH].rearrange("p (u n) -> p u n", n=CH),
                                            ACT.Exp).then_inc(s_e, 1)

                        @block.vector
                        def _(dve):
                            dve.sem_inc(s_e, 2)
                            dve.sem_inc(s_y, 4)
                            dve.sem_inc(s_yf, 2)
                            dve.sem_inc(s_st, 16)
                            with dve.Fori(0, NC // 2) as i:
                                for p in range(2):
                                    ns = bass.ds(i * 2 * CH + p * CH, CH)
                                    for t in range(CT):
                                        n = 2 * p + t
                                        dve.wait_ge(s_y, i * 4 + n + 5)
                                        nc.vector.scalar_tensor_tensor(
                                            out=z[:, t, :], in0=psOL[:, t * CH:(t + 1) * CH], scalar=sA[:, t, 1:2],
                                            in1=R1[:, ns], op0=ALU.mult, op1=ALU.mult).then_inc(s_yf, 1)
                                        dve.wait_ge(s_yf, i * 4 + n + 3)
                                        dve.wait_ge(s_st, i * 64 + 16 * (n + 1))
                                        nc.vector.scalar_tensor_tensor(
                                            out=res[:, t, :], in0=z[:, t, :], scalar=sA[:, t, 2:3],
                                            in1=X[:, t, ns], op0=ALU.add, op1=ALU.add).then_inc(s_res, 1)

                        @block.sync
                        def _(sp):
                            with sp.Fori(0, NC // 2) as i:
                                for p in range(2):
                                    for t in range(CT):
                                        sp.wait_ge(s_res, i * 4 + 2 * p + t + 1)
                                        sp.dma_start(out_v[b, :, t, bass.ds(i * 2 * CH + p * CH, CH)],
                                                     res[:, t, :]).then_inc(s_st, 16)
                            sp.wait_ge(s_st, 16 * (CT * NC + 1))
                    end_phase(c2, [s_s, s_e, s_y, s_yf, s_z, s_res, s_st])

        with nc.Fori(0, B) as b:
            layer0(b)
            layer1(b)


def kernel(**inputs):
    import numpy as _np
    import concourse.bacc as _bacc
    from concourse import mybir as _mybir
    from concourse.bass_utils import run_bass_kernel_spmd as _run

    names = ["x", "L0_conv_w_qkv", "L0_conv_w_proj", "L1_conv_g_w", "L1_conv_g_b", "L1_conv_theta_w",
             "L1_conv_theta_b", "L1_conv_phi_w", "L1_conv_phi_b", "L1_conv_W_w", "L1_conv_W_b", "L1_conv_bn_gamma",
             "L1_conv_bn_beta", "L1_conv_bn_mean", "L1_conv_bn_var"]
    nc = _bacc.Bacc("TRN2", target_bir_lowering=False, num_devices=1)
    arrays, args = {}, []
    for name in names:
        a = _np.asarray(inputs[name])
        if a.ndim == 2:
            a = a.T
        if a.ndim == 4:
            a = a.reshape(B, C, N)
        a = _np.ascontiguousarray(a)
        arrays[f"in_{name}"] = a
        args.append(nc.dram_tensor(f"in_{name}", a.shape, _mybir.dt.from_np(a.dtype), kind="ExternalInput").ap())
    args.append(nc.dram_tensor("out", (B, C, N), _mybir.dt.float32, kind="ExternalOutput").ap())
    args.append(nc.dram_tensor("att_out", (B, C, N), _mybir.dt.float32, kind="Internal").ap())
    args.append(nc.dram_tensor("att_sum", (B, HEADS, N), _mybir.dt.float32, kind="Internal").ap())
    args.append(nc.dram_tensor("att_inv", (B, HEADS, N), _mybir.dt.float32, kind="Internal").ap())
    conv_seq(nc, *args)
    r = _run(nc, [arrays], core_ids=[0])
    return r.results[0]["out"].reshape(B, C, H, W)
```

```python
from contextlib import ExitStack

import concourse.bass as bass
from concourse import mybir

ALU = mybir.AluOpType
ACT = mybir.ActivationFunctionType
AX = mybir.AxisListType
F32 = mybir.dt.float32
F16 = mybir.dt.float16
BF16 = mybir.dt.bfloat16
I32 = mybir.dt.int32

B, C, H, W = 2, 256, 64, 64
N = H * W
CT = C // 128
HEADS, D = 8, 32
G = 4
NG = HEADS // G
CH = 512
NC = N // CH
JT = N // 128
CM = C // 4
M = N // 4
MT = M // 128
EPS = 1e-5

QS = 16.0
MW = 1024.0
LIMIT = 60.0
SCORE = 1.0 / (QS * QS * float(D) ** 0.5)

RING = 4
SIZES = ([2, 2] * 15 + [2, 1, 1]) * 2
NBUF = 3
NOPS = len(SIZES)
UNITS = JT * G
STARTS = [sum(SIZES[:o]) for o in range(NOPS)]
SUM_PE = [7, 15, 23, 31]
SUM_V = [j for j in range(JT) if j not in SUM_PE]


def adds_through(j):
    k = sum(1 for t in SUM_V if t <= j)
    return 1 if k <= 2 else 2 if k <= 4 else k - 2


ADDS = adds_through(JT - 1)
DONE_BY = [next(o for o in range(NOPS) if STARTS[o] + SIZES[o] >= G * (j + 1)) for j in range(JT)]
VALUES_AT = [d + 1 for d in DONE_BY]
SUMS_AT = [DONE_BY[j] + 2 for j in SUM_PE]
ACC_AT = [NOPS - 1, NOPS + 2]
WORK = [(at, "values", j) for j, at in enumerate(VALUES_AT)]
WORK += [(at, "sums", j) for j, at in zip(SUM_PE, SUMS_AT)]
WORK += [(at, "acc", k) for k, at in enumerate(ACC_AT)]
TAIL = max(at for at, _, _ in WORK) + 1 - NOPS
ORDER = sorted((w for w in WORK if w[1] != "values"), key=lambda w: w[0])
FIRST_SUM, LAST_SUM = ORDER[0][1:], ORDER[-1][1:]
assert all(at >= DONE_BY[j] for at, what, j in WORK if what != "acc") and FIRST_SUM[0] == "sums"
assert ADDS % 2 == 0 and NOPS % NBUF == 0 and sum(SIZES) == UNITS and SUM_V[:4] == [0, 1, 2, 3]


def conv_seq(nc, x, wqkv, wproj, gw, gb, tw, tb, pw, pb, ww, wb, bn_g, bn_b, bn_m, bn_v, out, l_dram, r_dram):
    x_v = x.rearrange("b (t p) n -> b p t n", p=128)
    out_v = out.rearrange("b (t p) n -> b p t n", p=128)

    with ExitStack() as root:
        used = {}

        def unique(name):
            used[name] = used.get(name, 0) + 1
            return name if used[name] == 1 else f"{name}_{used[name]}"

        def sb(ctx, name, shape, dt=F32):
            return ctx.enter_context(nc.sbuf_tensor(unique(name), shape, dt))

        def sem(ctx, name):
            return ctx.enter_context(nc.semaphore(unique(name)))

        scores6 = root.enter_context(nc.psum_tensor("scores6", [128, 6 * CH], F32))
        bank = [scores6[:, i * 3 * CH:(i + 1) * 3 * CH] for i in range(2)]
        buf = [scores6[:, i * 2 * CH:(i + 1) * 2 * CH] for i in range(NBUF)]
        psOL = root.enter_context(nc.psum_tensor("psOL", [128, 2 * CH], F32))
        psO, psL = psOL[:, 0:CH], psOL[:, CH:2 * CH]

        def slot(i):
            return scores6[:, (i % 6) * CH:(i % 6 + 1) * CH]

        wq_sb = sb(root, "wq_sb", [128, CT, 3 * C])
        wp_sb = sb(root, "wp_sb", [128, CT, C])
        gw_sb = sb(root, "gw_sb", [128, CT, C])
        ww_sb = sb(root, "ww_sb", [128, CT, C])
        tw_sb = sb(root, "tw_sb", [128, CM])
        pw_sb = sb(root, "pw_sb", [128, CT, CM])
        col = sb(root, "col", [128, CT, 8])
        tb_sb = sb(root, "tb_sb", [CM, 2])
        sA = sb(root, "sA", [128, CT, 3])
        epsc = sb(root, "epsc", [128, 1])
        ident = sb(root, "ident", [128, 128])
        ones = sb(root, "ones", [128, D])
        X = sb(root, "X", [128, CT, N])
        O = sb(root, "O", [128, CT, N])
        heads = sb(root, "heads", [128, 128], BF16)
        safe = sb(root, "safe", [1, 1], I32)

        def end_phase(ctx, sems):
            with nc.Block() as block:
                @block.gpsimd
                def _(pool):
                    for s in sems:
                        pool.sem_clear(s)

        with ExitStack() as ctx:
            s_w = sem(ctx, "s_w")
            s_zero = sem(ctx, "s_zero")
            s_id = sem(ctx, "s_id")
            s_sq = sem(ctx, "s_sq")
            s_bn = sem(ctx, "s_bn")
            s_hd = sem(ctx, "s_hd")
            loads = [(wq_sb[:], wqkv.rearrange("(t p) o -> p t o", p=128)),
                     (wp_sb[:], wproj.rearrange("(t p) o -> p t o", p=128)),
                     (gw_sb[:], gw.rearrange("(t p) o -> p t o", p=128)),
                     (ww_sb[:], ww.rearrange("(t p) o -> p t o", p=128))]
            small = [(tw_sb[0:CM, :], tw), (pw_sb[CM:128, 0, :], pw[0:128 - CM, :]),
                     (pw_sb[:, 1, :], pw[128 - CM:, :]),
                     (tb_sb[:, 0:1], tb.rearrange("(p a) -> p a", a=1)),
                     (tb_sb[:, 1:2], pb.rearrange("(p a) -> p a", a=1))]
            for k, v in enumerate((gb, wb, bn_g, bn_b, bn_m, bn_v)):
                for t in range(CT):
                    small.append((col[:, t, k:k + 1], v[t * 128:(t + 1) * 128].rearrange("(p a) -> p a", a=1)))
            with nc.Block() as block:
                @block.sync
                def _(sp):
                    for dst, src in loads:
                        sp.dma_start(dst, src).then_inc(s_w, 16)
                    sp.wait_ge(s_zero, 2)
                    for dst, src in small:
                        sp.dma_start(dst, src).then_inc(s_w, 16)
                    sp.wait_ge(s_w, 16 * (len(loads) + len(small)))

                @block.gpsimd
                def _(pool):
                    nc.gpsimd.memset(ident[:], 0.0).then_inc(s_id, 1)
                    pool.wait_ge(s_id, 1)
                    nc.gpsimd.affine_select(out=ident[:], in_=ident[:], compare_op=ALU.not_equal, fill=1.0,
                                            base=0, pattern=[[-1, 128]], channel_multiplier=1).then_inc(s_id, 1)
                    pool.wait_ge(s_id, 2)

                @block.vector
                def _(dve):
                    nc.vector.memset(tw_sb[:], 0.0).then_inc(s_zero, 1)
                    nc.vector.memset(pw_sb[:, 0, :], 0.0).then_inc(s_zero, 1)
                    nc.vector.memset(ones[:], 1.0)
                    nc.vector.memset(heads[:], 0.0).then_inc(s_hd, 1)
                    dve.wait_ge(s_hd, 1)
                    for h in range(G):
                        last = nc.vector.memset(heads[h * D:(h + 1) * D, h * D:(h + 1) * D], 1.0)
                    last.then_inc(s_hd, 1)
                    dve.wait_ge(s_hd, 2)
                    dve.wait_ge(s_w, 16 * (len(loads) + len(small)))
                    nc.vector.tensor_scalar(sA[:, :, 0], col[:, :, 5], EPS, None, ALU.add).then_inc(s_bn, 1)
                    dve.wait_ge(s_bn, 1)
                    nc.vector.reciprocal(sA[:, :, 1], sA[:, :, 0]).then_inc(s_bn, 1)
                    dve.wait_ge(s_sq, 1)
                    nc.vector.tensor_tensor(sA[:, :, 1], sA[:, :, 0], col[:, :, 2], ALU.mult).then_inc(s_bn, 1)
                    nc.vector.tensor_tensor(col[:, :, 6], col[:, :, 1], col[:, :, 4], ALU.subtract).then_inc(s_bn, 1)
                    dve.wait_ge(s_bn, 4)
                    nc.vector.tensor_tensor(col[:, :, 7], col[:, :, 6], sA[:, :, 1], ALU.mult).then_inc(s_bn, 1)
                    dve.wait_ge(s_bn, 5)
                    nc.vector.tensor_tensor(sA[:, :, 2], col[:, :, 7], col[:, :, 3], ALU.add).then_inc(s_bn, 1)
                    dve.wait_ge(s_bn, 6)

                @block.scalar
                def _(act):
                    act.wait_ge(s_bn, 2)
                    nc.scalar.activation(sA[:, :, 0], sA[:, :, 1], ACT.Sqrt).then_inc(s_sq, 1)
            end_phase(ctx, [s_w, s_zero, s_id, s_sq, s_bn, s_hd])

        def layer0(b):
            with ExitStack() as ctx:
                Qst = sb(ctx, "Qst", [128, G, N], F16)
                Kst = sb(ctx, "Kst", [128, G, N], F16)
                V = sb(ctx, "V", [128, JT, G * D])
                s_x = [sem(ctx, f"s_x{c}") for c in range(NC)]
                s_pad = sem(ctx, "s_pad")
                s_mm = sem(ctx, "s_mm")
                s_ev = sem(ctx, "s_ev")
                s_hi = sem(ctx, "s_hi")
                for g in range(NG):
                    with ExitStack() as c2:
                        hi = [sb(c2, f"hi{k}", [128, N], F16) for k in range(2)]
                        lo = [sb(c2, f"lo{k}", [128, N], F16) for k in range(2)]
                        sq = [sb(c2, f"sq{k}", [128, CH], BF16) for k in range(2)]
                        nmax = sb(c2, "nmax", [128, 2 * NC])
                        bound = sb(c2, "bound", [128, 4])
                        s_st = sem(c2, "s_st")
                        s_sq = sem(c2, "s_sqr")
                        s_nm = sem(c2, "s_nm")
                        s_nx = sem(c2, "s_nx")
                        s_vm = sem(c2, "s_vm")
                        s_ve = sem(c2, "s_ve")
                        s_b = sem(c2, "s_b")
                        s_z = sem(c2, "s_z")
                        NU = 2 * NC
                        with nc.Block() as block:
                            @block.tensor
                            def _(pe):
                                def norms(u):
                                    pe.wait_ge(s_sq, u + 1)
                                    if u >= 1:
                                        pe.wait_ge(s_nx, u)
                                    nc.tensor.matmul(psL, heads[:], sq[u % 2][:], start=True, stop=True
                                                     ).then_inc(s_nm, 1)

                                for u in range(NU):
                                    k, c = divmod(u, NC)
                                    if u >= 6:
                                        pe.wait_ge(s_ev, u - 5)
                                    if g == 0 and k == 0:
                                        pe.wait_ge(s_x[c], 16)
                                    for t in range(CT):
                                        w = wq_sb[:, t, k * C + g * 128:k * C + (g + 1) * 128]
                                        last = nc.tensor.matmul(slot(u), w, X[:, t, c * CH:(c + 1) * CH],
                                                                start=(t == 0), stop=(t == CT - 1))
                                    last.then_inc(s_mm, 1)
                                    if u >= 2:
                                        norms(u - 2)
                                norms(NU - 2)
                                norms(NU - 1)
                                pe.wait_ge(s_ev, NU)
                                for q in range(JT // 4):
                                    if q >= 6:
                                        pe.wait_ge(s_ve, q - 5)
                                    for r in range(4):
                                        j = 4 * q + r
                                        for t in range(CT):
                                            last = nc.tensor.matmul(
                                                slot(q)[:, r * 128:(r + 1) * 128], X[:, t, j * 128:(j + 1) * 128],
                                                wq_sb[:, t, 2 * C + g * 128:2 * C + (g + 1) * 128],
                                                start=(t == 0), stop=(t == CT - 1))
                                    last.then_inc(s_vm, 1)
                                    if q == 1:
                                        pe.wait_ge(s_b, 2)
                                        nc.tensor.transpose(psO[0:1, 0:128], bound[:, 2:3], ident[:, :]).then_inc(s_nm, 1)

                            @block.scalar
                            def _(act):
                                for u in range(NU):
                                    k, c = divmod(u, NC)
                                    act.wait_ge(s_mm, u + 1)
                                    nc.scalar.activation(hi[k][:, c * CH:(c + 1) * CH], slot(u), ACT.Copy,
                                                         scale=QS).then_inc(s_hi, 1)
                                    if u >= 2:
                                        act.wait_ge(s_nm, u - 1)
                                    act.wait_ge(s_hi, u + 1)
                                    nc.scalar.activation(sq[u % 2][:], hi[k][:, c * CH:(c + 1) * CH], ACT.Square
                                                         ).then_inc(s_sq, 1)
                                for q in range(1, JT // 4, 2):
                                    act.wait_ge(s_vm, q + 1)
                                    act.wait_ge(s_ve, q)
                                    nc.scalar.copy(V[:, 4 * q:4 * q + 4, :].rearrange("p j n -> p (j n)"), slot(q)
                                                   ).then_inc(s_ve, 1)

                            @block.vector
                            def _(dve):
                                def largest(u):
                                    dve.wait_ge(s_nm, u + 1)
                                    nc.vector.tensor_reduce(nmax[:, u:u + 1], psL, AX.X, ALU.max).then_inc(s_nx, 1)

                                if g == 0:
                                    nc.vector.memset(Kst[96:128, :, :].bitcast(F32), 0.0).then_inc(s_pad, 1)
                                for u in range(NU):
                                    k, c = divmod(u, NC)
                                    dve.wait_ge(s_hi, u + 1)
                                    nc.vector.scalar_tensor_tensor(
                                        out=lo[k][:, c * CH:(c + 1) * CH], in0=slot(u), scalar=QS,
                                        in1=hi[k][:, c * CH:(c + 1) * CH],
                                        op0=ALU.mult, op1=ALU.subtract).then_inc(s_ev, 1)
                                    if u >= 2:
                                        largest(u - 2)
                                largest(NU - 2)
                                largest(NU - 1)
                                dve.wait_ge(s_nx, NU)
                                nc.vector.tensor_reduce(bound[:, 0:2], nmax[:].rearrange("p (k c) -> p k c", k=2),
                                                        AX.X, ALU.max).then_inc(s_b, 1)
                                dve.wait_ge(s_b, 1)
                                nc.vector.tensor_tensor(bound[:, 2:3], bound[:, 0:1], bound[:, 1:2], ALU.mult
                                                        ).then_inc(s_b, 1)
                                dve.wait_ge(s_nm, NU + 1)
                                nc.vector.tensor_reduce(bound[0:1, 3:4], psO[0:1, 0:128], AX.X, ALU.max).then_inc(s_b, 1)
                                dve.wait_ge(s_b, 3)
                                nc.vector.tensor_scalar(safe[:], bound[0:1, 3:4], (LIMIT / SCORE) ** 2, None, ALU.is_le
                                                        ).then_inc(s_b, 1)
                                for q in range(0, JT // 4, 2):
                                    dve.wait_ge(s_vm, q + 1)
                                    if q:
                                        dve.wait_ge(s_ve, q)
                                    nc.vector.tensor_copy(V[:, 4 * q:4 * q + 4, :].rearrange("p j n -> p (j n)"), slot(q)
                                                          ).then_inc(s_ve, 1)
                                dve.wait_ge(s_b, 4)

                            @block.gpsimd
                            def _(pool):
                                if g:
                                    nc.gpsimd.memset(Qst[96:97, :, :], 0.0).then_inc(s_z, 1)
                                else:
                                    nc.gpsimd.memset(Qst[96:128, :, :].bitcast(F32), 0.0).then_inc(s_z, 1)
                                    pool.wait_ge(s_pad, 1)
                                    nc.gpsimd.memset(Kst[96:97, :, :], MW).then_inc(s_pad, 1)
                                    pool.wait_ge(s_pad, 2)
                                pool.wait_ge(s_z, 1)

                            @block.sync
                            def _(sp):
                                if g == 0:
                                    for c in range(NC):
                                        sp.dma_start(X[:, :, c * CH:(c + 1) * CH], x_v[b, :, :, c * CH:(c + 1) * CH]
                                                     ).then_inc(s_x[c], 16)
                                n = 0
                                for k, dst, parts in ((0, Qst, (hi[0], lo[0], hi[0])), (1, Kst, (hi[1], hi[1], lo[1]))):
                                    sp.wait_ge(s_ev, NC * (k + 1))
                                    for h in range(G):
                                        for r, part in enumerate(parts):
                                            sp.dma_start(dst[r * D:(r + 1) * D, h, :],
                                                         part[h * D:(h + 1) * D, :]).then_inc(s_st, 16)
                                            n += 16
                                sp.wait_ge(s_st, n)
                        end_phase(c2, s_x + [s_pad, s_mm, s_ev, s_hi, s_st, s_sq, s_nm, s_nx, s_vm, s_ve, s_b, s_z])

                    known_safe = nc.values_load(safe[0:1, 0:1], min_val=0, max_val=1)
                    with ExitStack() as c2, nc.If(known_safe < 1):
                        mp = sb(c2, "mp", [128, G, JT, 3])
                        mcol = sb(c2, "mcol", [128, G * JT])
                        mrow = sb(c2, "mrow", [128, 128], F16)
                        s_s = sem(c2, "s_s")
                        s_m = sem(c2, "s_m")
                        s_t = sem(c2, "s_t")
                        s_r = sem(c2, "s_r")
                        parts = [(0, 3), (3, 6), (6, 8)]
                        n_it = G * len(parts)
                        with nc.Block() as block:
                            @block.gpsimd
                            def _(pool):
                                pool.sem_inc(s_m, 2)

                            @block.tensor
                            def _(pe):
                                with pe.Fori(0, JT) as it:
                                    for h in range(G):
                                        for k, (c0, c1) in enumerate(parts):
                                            o = h * 3 + k
                                            pe.wait_ge(s_m, it * n_it + o + 1)
                                            for c in range(c0, c1):
                                                last = nc.tensor.matmul(
                                                    bank[o % 2][:, (c - c0) * CH:(c - c0 + 1) * CH],
                                                    Qst[0:96, h, bass.ds(it * 128, 128)],
                                                    Kst[0:96, h, c * CH:(c + 1) * CH], start=True, stop=True)
                                            last.then_inc(s_s, 1)
                                pe.wait_ge(s_t, 1)
                                nc.tensor.transpose(psL[:, 0:128], mcol[:, :], ident[:, :]).then_inc(s_s, 1)

                            @block.vector
                            def _(dve):
                                with dve.Fori(0, JT) as it:
                                    for h in range(G):
                                        for k, (c0, c1) in enumerate(parts):
                                            o = h * 3 + k
                                            dve.wait_ge(s_s, it * n_it + o + 1)
                                            nc.vector.tensor_reduce(
                                                mp[:, h, bass.ds(it, 1), k], bank[o % 2][:, 0:(c1 - c0) * CH],
                                                AX.X, ALU.max).then_inc(s_m, 1)
                                dve.wait_ge(s_m, 2 + JT * n_it)
                                nc.vector.tensor_reduce(mcol[:, :], mp[:].rearrange("p h i k -> p (h i) k"),
                                                        AX.X, ALU.max).then_inc(s_t, 1)
                                dve.wait_ge(s_t, 1)

                            @block.scalar
                            def _(act):
                                act.wait_ge(s_s, JT * n_it + 1)
                                nc.scalar.mul(mrow[:, :], psL[:, 0:128], -1.0 / MW).then_inc(s_t, 1)

                            @block.sync
                            def _(sp):
                                sp.wait_ge(s_t, 2)
                                for h in range(G):
                                    sp.dma_start(Qst[96:97, h, :], mrow[h * JT:(h + 1) * JT, :]).then_inc(s_r, 16)
                                sp.wait_ge(s_r, 16 * G)
                        end_phase(c2, [s_s, s_m, s_t, s_r])

                    with ExitStack() as c2:
                        P = sb(c2, "P", [128, RING * G, CH])
                        acc = sb(c2, "acc", [128, 2, G, CH])
                        L = sb(c2, "L", [128, CH])
                        s_ready = sem(c2, "s_ready")
                        s_exp = sem(c2, "s_exp")
                        s_pv = sem(c2, "s_pv")
                        s_add = sem(c2, "s_add")
                        s_sum = sem(c2, "s_sum")
                        s_o_free = sem(c2, "s_o_free")
                        s_l_free = sem(c2, "s_l_free")
                        s_out = sem(c2, "s_out")

                        with nc.Block() as block:
                            @block.tensor
                            def _(pe):
                                def scores(before, o, c):
                                    if before is not None:
                                        pe.wait_ge(s_exp, before)
                                    for k in range(SIZES[o]):
                                        j, h = divmod(STARTS[o] + k, G)
                                        last = nc.tensor.matmul(buf[o % NBUF][:, k * CH:(k + 1) * CH],
                                                                Kst[:, h, j * 128:(j + 1) * 128],
                                                                Qst[:, h, bass.ds(c * CH, CH)], start=True, stop=True)
                                    last.then_inc(s_ready, 1)

                                def values(c, j):
                                    pe.wait_ge(s_exp, c * NOPS + DONE_BY[j] + 1)
                                    if j == 0:
                                        pe.wait_ge(s_o_free, c + 1)
                                    for h in range(G):
                                        last = nc.tensor.matmul(psO[h * D:(h + 1) * D, :],
                                                                V[:, j, h * D:(h + 1) * D],
                                                                P[:, (j % RING) * G + h, :],
                                                                start=(j == 0), stop=(j == JT - 1))
                                    last.then_inc(s_pv, 1)

                                def row_sums(c, what, j):
                                    if (what, j) == FIRST_SUM:
                                        pe.wait_ge(s_l_free, c + 1)
                                    if what == "acc":
                                        pe.wait_ge(s_add, (c + 2) * ADDS - 1 + j)
                                    for h in range(G):
                                        src = acc[:, j, h, :] if what == "acc" else P[:, (j % RING) * G + h, :]
                                        last = nc.tensor.matmul(psL[h * D:(h + 1) * D, :], ones[:], src,
                                                                start=(what, j) == FIRST_SUM,
                                                                stop=(what, j) == LAST_SUM)
                                    last.then_inc(s_sum, 1)

                                def work(c, at):
                                    for when, what, j in WORK:
                                        if when == at:
                                            values(c, j) if what == "values" else row_sums(c, what, j)

                                def inside(c, last):
                                    for o in range(TAIL, NOPS + TAIL):
                                        if o + NBUF < NOPS:
                                            scores(c * NOPS + o + 1, o + NBUF, c)
                                        elif not last:
                                            scores(c * NOPS + o + 1, o + NBUF - NOPS, c + 1)
                                        work(c, o)
                                        if o >= NOPS and not last:
                                            work(c + 1, o - NOPS)

                                for o in range(NBUF):
                                    scores(None, o, 0)
                                for o in range(TAIL):
                                    scores(o + 1, o + NBUF, 0)
                                    work(0, o)
                                with pe.Fori(0, NC - 1) as c:
                                    inside(c, False)
                                inside(NC - 1, True)

                            @block.scalar
                            def _(act):
                                with act.Fori(0, NC) as c:
                                    for o in range(NOPS):
                                        act.wait_ge(s_ready, c * NOPS + o + 1)
                                        u0 = STARTS[o]
                                        j0, j1 = u0 // G, (u0 + SIZES[o] - 1) // G
                                        if j0 != j1 or u0 % G == 0:
                                            act.wait_ge(s_pv, c * JT + j1 + 1)
                                            before = (j1 - RING) % JT
                                            if before in SUM_PE:
                                                n = ORDER.index((SUMS_AT[SUM_PE.index(before)], "sums", before)) + 1
                                                act.wait_ge(s_sum, (c + (j1 >= RING)) * len(ORDER) + n)
                                            if j1 >= RING:
                                                act.wait_ge(s_add, (c + 1) * ADDS + adds_through(j1 - RING))
                                            else:
                                                act.wait_ge(s_add, c * ADDS + adds_through(j1 - RING + JT))
                                        r = u0 % (RING * G)
                                        s3 = buf[o % NBUF][:, 0:SIZES[o] * CH].rearrange("p (u n) -> p u n", n=CH)
                                        nc.scalar.activation(P[:, r:r + SIZES[o], :], s3, ACT.Exp,
                                                             scale=SCORE).then_inc(s_exp, 1)

                            @block.vector
                            def _(dve):
                                dve.sem_inc(s_pv, RING)
                                dve.sem_inc(s_add, ADDS)
                                dve.sem_inc(s_sum, len(ORDER))
                                dve.sem_inc(s_o_free, 1)
                                dve.sem_inc(s_l_free, 1)
                                dve.sem_inc(s_out, 16)

                                def sums_out(c):
                                    dve.wait_ge(s_sum, (c + 2) * len(ORDER))
                                    dve.wait_ge(s_out, 16 * (c + 1))
                                    nc.vector.tensor_copy(L[:], psL).then_inc(s_l_free, 1)

                                def chunk(c, first):
                                    for n in range(ADDS):
                                        j = SUM_V[2 * n + 1] if n < 2 else SUM_V[n + 2]
                                        dve.wait_ge(s_exp, c * NOPS + DONE_BY[j] + 1)
                                        new = P[:, (j % RING) * G:(j % RING + 1) * G, :]
                                        if n < 2:
                                            dve.wait_ge(s_sum, c * len(ORDER) + ORDER.index((ACC_AT[n], "acc", n)) + 1)
                                            j0 = SUM_V[2 * n]
                                            old = P[:, (j0 % RING) * G:(j0 % RING + 1) * G, :]
                                        else:
                                            dve.wait_ge(s_add, (c + 1) * ADDS + n - 1)
                                            old = acc[:, n % 2]
                                        nc.vector.tensor_tensor(acc[:, n % 2], old, new, ALU.add).then_inc(s_add, 1)
                                        if n == 1 and not first:
                                            sums_out(c - 1)
                                    dve.wait_ge(s_pv, RING + (c + 1) * JT)
                                    nc.vector.tensor_copy(O[:, g, bass.ds(c * CH, CH)], psO).then_inc(s_o_free, 1)

                                chunk(0, True)
                                with dve.Fori(1, NC) as c:
                                    chunk(c, False)
                                sums_out(NC - 1)

                            @block.sync
                            def _(sp):
                                with sp.Fori(0, NC) as c:
                                    sp.wait_ge(s_l_free, c + 2)
                                    sp.dma_start(l_dram[b, g * G:(g + 1) * G, bass.ds(c * CH, CH)],
                                                 L[0:128:D, :]).then_inc(s_out, 16)
                                sp.wait_ge(s_out, 16 * (NC + 1))
                        end_phase(c2, [s_ready, s_exp, s_pv, s_add, s_sum, s_o_free, s_l_free, s_out])

        def layer1(b):
            with ExitStack() as ctx:
                T = sb(ctx, "T", [128, N])
                s_rec = sem(ctx, "s_rec")
                s_mm = sem(ctx, "s_mm1")
                s_ev = sem(ctx, "s_ev1")
                with ExitStack() as c2:
                    R = sb(c2, "R", [128, CT, N])
                    L = sb(c2, "L", [128, HEADS * N // 128])
                    Li = sb(c2, "Li", [128, HEADS * N // 128])
                    s_l = sem(c2, "s_l")
                    s_norm = sem(c2, "s_norm")
                    s_r4 = [sem(c2, f"s_r4{q}") for q in range(4)]
                    QN = N // 4
                    with nc.Block() as block:
                        @block.sync
                        def _(sp):
                            sp.dma_start(L[:], l_dram[b].rearrange("h (a n) -> (h a) n", n=HEADS * N // 128)
                                         ).then_inc(s_l, 16)
                            sp.wait_ge(s_rec, 1)
                            sp.dma_start(r_dram[b].rearrange("h (a n) -> (h a) n", n=HEADS * N // 128),
                                         Li[:]).then_inc(s_l, 16)
                            sp.wait_ge(s_l, 32)
                            for q in range(4):
                                for h in range(HEADS):
                                    sp.dma_start(R[h % G * D:(h % G + 1) * D, h // G, q * QN:(q + 1) * QN],
                                                 r_dram[b, h:h + 1, q * QN:(q + 1) * QN].broadcast_to([D, QN])
                                                 ).then_inc(s_r4[q], 16)

                        @block.vector
                        def _(dve):
                            dve.wait_ge(s_l, 16)
                            nc.vector.reciprocal(Li[:], L[:]).then_inc(s_rec, 1)
                            def normalise(c):
                                cs = slice(c * CH, (c + 1) * CH)
                                dve.wait_ge(s_r4[c // 2], 16 * HEADS)
                                nc.vector.tensor_tensor(O[:, :, cs], O[:, :, cs], R[:, :, cs], ALU.mult
                                                        ).then_inc(s_norm, 1)

                            normalise(0)
                            for u in range(NC * CT):
                                c, t = divmod(u, CT)
                                if t == 0 and c + 1 < NC:
                                    normalise(c + 1)
                                cs = slice(c * CH, (c + 1) * CH)
                                dve.wait_ge(s_mm, u + 1)
                                nc.vector.tensor_tensor(X[:, t, cs], X[:, t, cs], slot(u), ALU.add
                                                        ).then_inc(s_ev, 1)
                            dve.wait_ge(s_ev, NC * CT)

                        @block.tensor
                        def _(pe):
                            for u in range(NC * CT):
                                c, t = divmod(u, CT)
                                pe.wait_ge(s_norm, c + 1)
                                if u >= 6:
                                    pe.wait_ge(s_ev, u - 5)
                                for k in range(CT):
                                    last = nc.tensor.matmul(slot(u), wp_sb[:, k, t * 128:(t + 1) * 128],
                                                            O[:, k, c * CH:(c + 1) * CH],
                                                            start=(k == 0), stop=(k == CT - 1))
                                last.then_inc(s_mm, 1)
                    end_phase(c2, [s_rec, s_mm, s_ev, s_l, s_norm] + s_r4)

                Ph = sb(ctx, "Ph", [128, M])
                GT = sb(ctx, "GT", [128, MT, C])
                s_pad = sem(ctx, "s_pad1")
                with ExitStack() as c2:
                    Gp = sb(c2, "Gp", [128, CT, M])
                    pooled = sb(c2, "pooled", [128, 2, CH // 4])
                    s_pool = sem(c2, "s_pool")
                    UN = 4
                    with nc.Block() as block:
                        @block.gpsimd
                        def _(pool):
                            nc.gpsimd.memset(T[CM:128, :], 0.0)
                            nc.gpsimd.memset(Ph[CM:128, :], 0.0).then_inc(s_pad, 1)
                            pool.wait_ge(s_pad, 1)
                            nc.gpsimd.memset(Ph[CM:CM + 1, :], 1.0).then_inc(s_pad, 1)
                            pool.wait_ge(s_pad, 2)

                        @block.tensor
                        def _(pe):
                            for u in range(UN * NC):
                                c, k = divmod(u, UN)
                                cs = slice(c * CH, (c + 1) * CH)
                                if u >= 6:
                                    pe.wait_ge(s_ev, u - 5)
                                if k == 0:
                                    last = nc.tensor.matmul(slot(u)[0:CM, :], tw_sb[:], X[:, 0, cs], start=True, stop=True)
                                else:
                                    for t in range(CT):
                                        w = pw_sb[:, t, :] if k == 1 else gw_sb[:, t, (k - 2) * 128:(k - 1) * 128]
                                        last = nc.tensor.matmul(slot(u)[0:CM if k == 1 else 128, :], w, X[:, t, cs],
                                                                start=(t == 0), stop=(t == CT - 1))
                                last.then_inc(s_mm, 1)
                            pe.wait_ge(s_ev, UN * NC)
                            for m in range(MT):
                                if m >= 6:
                                    pe.wait_ge(s_ev, UN * NC + m - 5)
                                for t in range(CT):
                                    last = nc.tensor.matmul(slot(m)[:, 0:C], Gp[:, t, m * 128:(m + 1) * 128],
                                                            ww_sb[:, t, :], start=(t == 0), stop=(t == CT - 1))
                                last.then_inc(s_mm, 1)

                        @block.vector
                        def _(dve):
                            pools = 0
                            for u in range(UN * NC):
                                c, k = divmod(u, UN)
                                dve.wait_ge(s_mm, u + 1)
                                if k == 0:
                                    nc.vector.tensor_scalar(T[0:CM, c * CH:(c + 1) * CH], slot(u)[0:CM, :],
                                                            tb_sb[:, 0:1], None, ALU.add).then_inc(s_ev, 1)
                                    continue
                                P0 = CM if k == 1 else 128
                                q = CH // 4
                                tmp = pooled[0:P0, pools % 2, :]
                                src = slot(u)[0:P0, :].rearrange("p (a u b v) -> p a b u v", u=2, v=2, b=W // 2)
                                nc.vector.tensor_reduce(tmp.rearrange("p (a b) -> p a b", b=W // 2), src, AX.XY,
                                                        ALU.max).then_inc(s_pool, 1)
                                pools += 1
                                dve.wait_ge(s_pool, pools)
                                dst = Ph[0:CM, c * q:(c + 1) * q] if k == 1 else Gp[:, k - 2, c * q:(c + 1) * q]
                                bias = tb_sb[:, 1:2] if k == 1 else col[:, k - 2, 0:1]
                                nc.vector.tensor_scalar(dst, tmp, bias, None, ALU.add).then_inc(s_ev, 1)
                            for m in range(MT):
                                dve.wait_ge(s_mm, UN * NC + m + 1)
                                nc.vector.tensor_copy(GT[:, m, :], slot(m)[:, 0:C]).then_inc(s_ev, 1)
                            dve.wait_ge(s_ev, UN * NC + MT)
                    end_phase(c2, [s_pad, s_pool, s_mm, s_ev])

                R1 = sb(ctx, "R1", [128, N])
                with ExitStack() as c2:
                    stat = sb(c2, "stat", [128, 2, JT])
                    mx = sb(c2, "mx", [128, JT])
                    l1 = sb(c2, "l1", [128, JT])
                    junk = sb(c2, "junk", [128, M])
                    statT = sb(c2, "statT", [2 * JT, 128])
                    s_e = sem(c2, "s_e")
                    s_n = sem(c2, "s_n")
                    s_row = sem(c2, "s_row")
                    with nc.Block() as block:
                        @block.tensor
                        def _(pe):
                            for i in range(JT):
                                if i >= 2:
                                    pe.wait_ge(s_e, i - 1)
                                for k in range(M // CH):
                                    last = nc.tensor.matmul(bank[i % 2][:, k * CH:(k + 1) * CH],
                                                            T[:, i * 128:(i + 1) * 128],
                                                            Ph[:, k * CH:(k + 1) * CH], start=True, stop=True)
                                last.then_inc(s_mm, 1)
                            pe.wait_ge(s_n, JT + 1)
                            nc.tensor.transpose(psL[0:2 * JT, 0:128], stat[:].rearrange("p k i -> p (k i)"),
                                                ident[:, :]).then_inc(s_mm, 1)

                        @block.vector
                        def _(dve):
                            for i in range(JT):
                                dve.wait_ge(s_mm, i + 1)
                                nc.vector.tensor_reduce(mx[:, i:i + 1], bank[i % 2][:, 0:M], AX.X, ALU.max
                                                        ).then_inc(s_ev, 1)
                                dve.wait_ge(s_ev, i + 1)
                                nc.vector.tensor_scalar(stat[:, 0, i:i + 1], mx[:, i:i + 1], -1.0, None, ALU.mult
                                                        ).then_inc(s_n, 1)
                            dve.wait_ge(s_e, JT)
                            nc.vector.reciprocal(stat[:, 1, :], l1[:]).then_inc(s_n, 1)
                            dve.wait_ge(s_mm, JT + 1)
                            nc.vector.tensor_copy(statT[:], psL[0:2 * JT, 0:128]).then_inc(s_n, 1)

                        @block.scalar
                        def _(act):
                            for i in range(JT):
                                act.wait_ge(s_n, i + 1)
                                if i:
                                    act.wait_ge(s_e, i)
                                nc.scalar.activation(junk[:], bank[i % 2][:, 0:M], ACT.Exp, bias=stat[:, 0, i:i + 1],
                                                     accum_out=l1[:, i:i + 1]).then_inc(s_e, 1)

                        @block.sync
                        def _(sp):
                            sp.wait_ge(s_n, JT + 2)
                            sp.dma_start(T[CM:CM + 1, :], statT[0:JT, :]).then_inc(s_row, 16)
                            sp.dma_start(r_dram[b, 0:1, :].rearrange("a (i n) -> (a i) n", n=128),
                                         statT[JT:2 * JT, :]).then_inc(s_row, 16)
                            sp.wait_ge(s_row, 32)
                            sp.dma_start(R1[:], r_dram[b, 0:1, :].broadcast_to([128, N])).then_inc(s_row, 16)
                            sp.wait_ge(s_row, 48)
                    end_phase(c2, [s_mm, s_ev, s_e, s_n, s_row])

                with ExitStack() as c2:
                    PT = sb(c2, "PT", [128, 2, MT, CH])
                    z = sb(c2, "z", [128, 2, CH])
                    res = sb(c2, "res", [128, 2, CH])
                    s_s = sem(c2, "s_s1")
                    s_e = sem(c2, "s_e1")
                    s_y = sem(c2, "s_y")
                    s_yf = sem(c2, "s_yf")
                    s_z = sem(c2, "s_z")
                    s_res = sem(c2, "s_res")
                    s_st = sem(c2, "s_st1")
                    SZ = [3, 3, 2]
                    with nc.Block() as block:
                        @block.tensor
                        def _(pe):
                            with pe.Fori(0, NC // 2) as i:
                                for p in range(2):
                                    for k in range(3):
                                        o = 3 * p + k
                                        pe.wait_ge(s_e, i * 6 + o + 1)
                                        for r in range(SZ[k]):
                                            m = 3 * k + r
                                            last = nc.tensor.matmul(bank[o % 2][:, r * CH:(r + 1) * CH],
                                                                    Ph[:, m * 128:(m + 1) * 128],
                                                                    T[:, bass.ds(i * 2 * CH + p * CH, CH)],
                                                                    start=True, stop=True)
                                        last.then_inc(s_s, 1)
                                for p in range(2):
                                    pe.wait_ge(s_e, i * 6 + 3 * p + 5)
                                    for t in range(CT):
                                        pe.wait_ge(s_yf, i * 4 + 2 * p + t + 1)
                                        for m in range(MT):
                                            last = nc.tensor.matmul(psOL[:, t * CH:(t + 1) * CH],
                                                                    GT[:, m, t * 128:(t + 1) * 128],
                                                                    PT[:, p, m, :], start=(m == 0), stop=(m == MT - 1))
                                        last.then_inc(s_y, 1)

                        @block.scalar
                        def _(act):
                            with act.Fori(0, NC // 2) as i:
                                for p in range(2):
                                    act.wait_ge(s_y, i * 4 + 2 * p + 2)
                                    for k in range(3):
                                        o = 3 * p + k
                                        act.wait_ge(s_s, i * 6 + o + 1)
                                        nc.scalar.activation(
                                            PT[:, p, 3 * k:3 * k + SZ[k], :],
                                            bank[o % 2][:, 0:SZ[k] * CH].rearrange("p (u n) -> p u n", n=CH),
                                            ACT.Exp).then_inc(s_e, 1)

                        @block.vector
                        def _(dve):
                            dve.sem_inc(s_e, 2)
                            dve.sem_inc(s_y, 4)
                            dve.sem_inc(s_yf, 2)
                            dve.sem_inc(s_st, 16)
                            with dve.Fori(0, NC // 2) as i:
                                for p in range(2):
                                    ns = bass.ds(i * 2 * CH + p * CH, CH)
                                    for t in range(CT):
                                        n = 2 * p + t
                                        dve.wait_ge(s_y, i * 4 + n + 5)
                                        nc.vector.scalar_tensor_tensor(
                                            out=z[:, t, :], in0=psOL[:, t * CH:(t + 1) * CH], scalar=sA[:, t, 1:2],
                                            in1=R1[:, ns], op0=ALU.mult, op1=ALU.mult).then_inc(s_yf, 1)
                                        dve.wait_ge(s_yf, i * 4 + n + 3)
                                        dve.wait_ge(s_st, i * 64 + 16 * (n + 1))
                                        nc.vector.scalar_tensor_tensor(
                                            out=res[:, t, :], in0=z[:, t, :], scalar=sA[:, t, 2:3],
                                            in1=X[:, t, ns], op0=ALU.add, op1=ALU.add).then_inc(s_res, 1)

                        @block.sync
                        def _(sp):
                            with sp.Fori(0, NC // 2) as i:
                                for p in range(2):
                                    for t in range(CT):
                                        sp.wait_ge(s_res, i * 4 + 2 * p + t + 1)
                                        sp.dma_start(out_v[b, :, t, bass.ds(i * 2 * CH + p * CH, CH)],
                                                     res[:, t, :]).then_inc(s_st, 16)
                            sp.wait_ge(s_st, 16 * (CT * NC + 1))
                    end_phase(c2, [s_s, s_e, s_y, s_yf, s_z, s_res, s_st])

        with nc.Fori(0, B) as b:
            layer0(b)
            layer1(b)


def kernel(**inputs):
    import numpy as _np
    import concourse.bacc as _bacc
    from concourse import mybir as _mybir
    from concourse.bass_utils import run_bass_kernel_spmd as _run

    names = ["x", "L0_conv_w_qkv", "L0_conv_w_proj", "L1_conv_g_w", "L1_conv_g_b", "L1_conv_theta_w",
             "L1_conv_theta_b", "L1_conv_phi_w", "L1_conv_phi_b", "L1_conv_W_w", "L1_conv_W_b", "L1_conv_bn_gamma",
             "L1_conv_bn_beta", "L1_conv_bn_mean", "L1_conv_bn_var"]
    nc = _bacc.Bacc("TRN2", target_bir_lowering=False, num_devices=1)
    arrays, args = {}, []
    for name in names:
        a = _np.asarray(inputs[name])
        if a.ndim == 2:
            a = a.T
        if a.ndim == 4:
            a = a.reshape(B, C, N)
        a = _np.ascontiguousarray(a)
        arrays[f"in_{name}"] = a
        args.append(nc.dram_tensor(f"in_{name}", a.shape, _mybir.dt.from_np(a.dtype), kind="ExternalInput").ap())
    args.append(nc.dram_tensor("out", (B, C, N), _mybir.dt.float32, kind="ExternalOutput").ap())
    args.append(nc.dram_tensor("att_sum", (B, HEADS, N), _mybir.dt.float32, kind="Internal").ap())
    args.append(nc.dram_tensor("att_inv", (B, HEADS, N), _mybir.dt.float32, kind="Internal").ap())
    conv_seq(nc, *args)
    r = _run(nc, [arrays], core_ids=[0])
    return r.results[0]["out"].reshape(B, C, H, W)
```

```python
from contextlib import ExitStack

import concourse.bass as bass
from concourse import mybir

ALU = mybir.AluOpType
ACT = mybir.ActivationFunctionType
AX = mybir.AxisListType
F32 = mybir.dt.float32
F16 = mybir.dt.float16
BF16 = mybir.dt.bfloat16
I32 = mybir.dt.int32

B, C, H, W = 2, 256, 64, 64
N = H * W
CT = C // 128
HEADS, D = 8, 32
G = 4
NG = HEADS // G
CH = 512
NC = N // CH
JT = N // 128
CM = C // 4
M = N // 4
MT = M // 128
LP = G * CH // 128
EPS = 1e-5

QS = 16.0
MW = 1024.0
MW1 = 256.0
SCORE1 = 1.0 / (QS * QS)
PS = 1024.0
WS = 256.0
YS = 1.0 / (QS * WS)
LIMIT = 60.0
SCORE = 1.0 / (QS * QS * float(D) ** 0.5)

RING = 4
SIZES = ([2, 2] * 15 + [2, 1, 1]) * 2
NBUF = 3
NOPS = len(SIZES)
UNITS = JT * G
STARTS = [sum(SIZES[:o]) for o in range(NOPS)]
SUM_PE = [9, 20, 31]
SUM_V = [j for j in range(JT) if j not in SUM_PE]


def adds_through(j):
    k = sum(1 for t in SUM_V if t <= j)
    return 1 if k <= 2 else 2 if k <= 4 else k - 2


ADDS = adds_through(JT - 1)


def sum_of(n):
    return n % 2 if n < 2 else (n + ADDS) % 2


DONE_BY = [next(o for o in range(NOPS) if STARTS[o] + SIZES[o] >= G * (j + 1)) for j in range(JT)]
VALUES_AT = [d + 1 for d in DONE_BY]
SUMS_AT = [DONE_BY[j] + 2 for j in SUM_PE]
ACC_AT = [NOPS + 1, NOPS + 3]
O_AT, L_AT = 3, 8
WORK = [(at, "values", j) for j, at in enumerate(VALUES_AT)]
WORK += [(at, "sums", j) for j, at in zip(SUM_PE, SUMS_AT)]
WORK += [(at, "acc", k) for k, at in enumerate(ACC_AT)]
TAIL = max(at for at, _, _ in WORK) + 1 - NOPS
ORDER = sorted((w for w in WORK if w[1] != "values"), key=lambda w: w[0])
FIRST_SUM, LAST_SUM = ORDER[0][1:], ORDER[-1][1:]
assert all(at >= DONE_BY[j] for at, what, j in WORK if what != "acc") and FIRST_SUM[0] == "sums"
assert NOPS % NBUF == 0 and sum(SIZES) == UNITS and SUM_V[:4] == [0, 1, 2, 3]


def conv_seq(nc, x, wqkv, wproj, gw, tw, pw, ww, vectors, biases, out, r_dram, r1_dram):
    x_v = x.rearrange("b (t p) n -> b p t n", p=128)
    out_v = out.rearrange("b (t p) n -> b p t n", p=128)

    with ExitStack() as root:
        used = {}

        def unique(name):
            used[name] = used.get(name, 0) + 1
            return name if used[name] == 1 else f"{name}_{used[name]}"

        def sb(ctx, name, shape, dt=F32):
            return ctx.enter_context(nc.sbuf_tensor(unique(name), shape, dt))

        def sem(ctx, name):
            return ctx.enter_context(nc.semaphore(unique(name)))

        scores6 = root.enter_context(nc.psum_tensor("scores6", [128, 6 * CH], F32))
        bank = [scores6[:, i * 3 * CH:(i + 1) * 3 * CH] for i in range(2)]
        buf = [scores6[:, i * 2 * CH:(i + 1) * 2 * CH] for i in range(NBUF)]
        psOL = root.enter_context(nc.psum_tensor("psOL", [128, 2 * CH], F32))
        psO, psL = psOL[:, 0:CH], psOL[:, CH:2 * CH]

        def slot(i):
            return scores6[:, (i % 6) * CH:(i % 6 + 1) * CH]

        wq_sb = sb(root, "wq_sb", [128, CT, 3 * C])
        wp_sb = sb(root, "wp_sb", [128, CT, C])
        cw = [sb(root, f"cw_{n}", [128, CT, CM + CM + C], F16) for n in ("hi", "lo")]
        col = sb(root, "col", [128, CT, 8])
        tb_sb = sb(root, "tb_sb", [CM, 2])
        sA = sb(root, "sA", [128, CT, 4])
        epsc = sb(root, "epsc", [128, 1])
        ident = sb(root, "ident", [128, 128])
        ones = sb(root, "ones", [128, D])
        X = sb(root, "X", [128, CT, N])
        O = sb(root, "O", [128, CT, N])
        heads = sb(root, "heads", [128, 128], BF16)
        safe = sb(root, "safe", [1, 1], I32)
        L = sb(root, "L", [128, CH])
        Ls = sb(root, "Ls", [128, NG, NC, LP])

        def end_phase(ctx, sems):
            with nc.Block() as block:
                @block.gpsimd
                def _(pool):
                    for s in sems[0::5]:
                        pool.sem_clear(s)

                @block.vector
                def _(dve):
                    for s in sems[1::5]:
                        dve.sem_clear(s)

                @block.scalar
                def _(act):
                    for s in sems[2::5]:
                        act.sem_clear(s)

                @block.tensor
                def _(pe):
                    for s in sems[3::5]:
                        pe.sem_clear(s)

                @block.sync
                def _(sp):
                    for s in sems[4::5]:
                        sp.sem_clear(s)

        with ExitStack() as ctx:
            cw32 = sb(ctx, "cw32", [128, CT, CM + CM + C])
            tw_sb, pw_sb, gw_sb = cw32[:, 0, 0:CM], cw32[:, :, CM:2 * CM], cw32[:, :, 2 * CM:]
            s_cw = sem(ctx, "s_cw")
            s_w = sem(ctx, "s_w")
            s_zero = sem(ctx, "s_zero")
            s_id = sem(ctx, "s_id")
            s_sq = sem(ctx, "s_sq")
            s_bn = sem(ctx, "s_bn")
            s_hd = sem(ctx, "s_hd")
            loads = [(wq_sb[:], wqkv.rearrange("(t p) o -> p t o", p=128)),
                     (wp_sb[:], wproj.rearrange("(t p) o -> p t o", p=128)),
                     (gw_sb, gw.rearrange("(t p) o -> p t o", p=128)),
                     (col[:, :, 0:6], vectors.rearrange("(t p) k -> p t k", p=128)),
                     (tb_sb[:], biases)]
            small = [(tw_sb[0:CM, :], tw), (pw_sb[CM:128, 0, :], pw[0:128 - CM, :]),
                     (pw_sb[:, 1, :], pw[128 - CM:, :])]
            with nc.Block() as block:
                @block.sync
                def _(sp):
                    for dst, src in loads:
                        sp.dma_start(dst, src).then_inc(s_w, 16)
                    sp.wait_ge(s_zero, 2)
                    for dst, src in small:
                        sp.dma_start(dst, src).then_inc(s_w, 16)
                    sp.wait_ge(s_w, 16 * (len(loads) + len(small)))

                @block.gpsimd
                def _(pool):
                    nc.gpsimd.memset(ident[:], 0.0).then_inc(s_id, 1)
                    pool.wait_ge(s_id, 1)
                    nc.gpsimd.affine_select(out=ident[:], in_=ident[:], compare_op=ALU.not_equal, fill=1.0,
                                            base=0, pattern=[[-1, 128]], channel_multiplier=1).then_inc(s_id, 1)
                    pool.wait_ge(s_id, 2)

                @block.vector
                def _(dve):
                    nc.vector.memset(cw32[:, :, 0:CM], 0.0).then_inc(s_zero, 1)
                    nc.vector.memset(pw_sb[:, 0, :], 0.0).then_inc(s_zero, 1)
                    nc.vector.memset(ones[:], 1.0)
                    nc.vector.memset(heads[:], 0.0).then_inc(s_hd, 1)
                    dve.wait_ge(s_hd, 1)
                    for h in range(G):
                        last = nc.vector.memset(heads[h * D:(h + 1) * D, h * D:(h + 1) * D], 1.0)
                    last.then_inc(s_hd, 1)
                    dve.wait_ge(s_hd, 2)
                    dve.wait_ge(s_w, 16 * (len(loads) + len(small)))
                    dve.wait_ge(s_cw, 1)
                    nc.vector.scalar_tensor_tensor(out=cw[1][:], in0=cw32[:], scalar=WS, in1=cw[0][:],
                                                   op0=ALU.mult, op1=ALU.subtract).then_inc(s_cw, 1)
                    dve.wait_ge(s_cw, 2)
                    nc.vector.tensor_scalar(sA[:, :, 0], col[:, :, 5], EPS, None, ALU.add).then_inc(s_bn, 1)
                    dve.wait_ge(s_bn, 1)
                    nc.vector.reciprocal(sA[:, :, 1], sA[:, :, 0]).then_inc(s_bn, 1)
                    dve.wait_ge(s_sq, 1)
                    nc.vector.tensor_tensor(sA[:, :, 1], sA[:, :, 0], col[:, :, 2], ALU.mult).then_inc(s_bn, 1)
                    nc.vector.tensor_tensor(col[:, :, 6], col[:, :, 1], col[:, :, 4], ALU.subtract).then_inc(s_bn, 1)
                    dve.wait_ge(s_bn, 4)
                    nc.vector.tensor_tensor(col[:, :, 7], col[:, :, 6], sA[:, :, 1], ALU.mult).then_inc(s_bn, 1)
                    dve.wait_ge(s_bn, 5)
                    nc.vector.tensor_tensor(sA[:, :, 2], col[:, :, 7], col[:, :, 3], ALU.add).then_inc(s_bn, 1)
                    nc.vector.tensor_scalar(sA[:, :, 3], sA[:, :, 1], 1.0 / (PS * QS), None, ALU.mult).then_inc(s_bn, 1)
                    dve.wait_ge(s_bn, 7)

                @block.scalar
                def _(act):
                    act.wait_ge(s_w, 16 * (len(loads) + len(small)))
                    nc.scalar.activation(cw[0][:], cw32[:], ACT.Copy, scale=WS).then_inc(s_cw, 1)
                    act.wait_ge(s_bn, 2)
                    nc.scalar.activation(sA[:, :, 0], sA[:, :, 1], ACT.Sqrt).then_inc(s_sq, 1)
            end_phase(ctx, [s_cw, s_w, s_zero, s_id, s_sq, s_bn, s_hd])

        def layer0(b):
            with ExitStack() as ctx:
                Qst = sb(ctx, "Qst", [128, G, N], F16)
                Kst = sb(ctx, "Kst", [128, G, N], F16)
                V = sb(ctx, "V", [128, JT, G * D])
                s_x = [sem(ctx, f"s_x{c}") for c in range(NC)]
                s_pad = sem(ctx, "s_pad")
                s_mm = sem(ctx, "s_mm")
                s_ev = sem(ctx, "s_ev")
                s_hi = sem(ctx, "s_hi")
                for g in range(NG):
                    with ExitStack() as c2:
                        hi = [sb(c2, f"hi{k}", [128, N], F16) for k in range(2)]
                        lo = [sb(c2, f"lo{k}", [128, N], F16) for k in range(2)]
                        sq = [sb(c2, f"sq{k}", [128, CH], BF16) for k in range(2)]
                        nmax = sb(c2, "nmax", [128, 2 * NC])
                        bound = sb(c2, "bound", [128, 4])
                        s_st = sem(c2, "s_st")
                        s_sq = sem(c2, "s_sqr")
                        s_nm = sem(c2, "s_nm")
                        s_nx = sem(c2, "s_nx")
                        s_vm = sem(c2, "s_vm")
                        s_ve = sem(c2, "s_ve")
                        s_b = sem(c2, "s_b")
                        s_z = sem(c2, "s_z")
                        NU = 2 * NC
                        with nc.Block() as block:
                            @block.tensor
                            def _(pe):
                                def norms(u):
                                    pe.wait_ge(s_sq, u + 1)
                                    if u >= 2:
                                        pe.wait_ge(s_nx, u - 1)
                                    nc.tensor.matmul((psO, psL)[u % 2], heads[:], sq[u % 2][:], start=True, stop=True
                                                     ).then_inc(s_nm, 1)

                                for u in range(NU):
                                    k, c = divmod(u, NC)
                                    if u >= 6:
                                        pe.wait_ge(s_ev, u - 5)
                                    if g == 0 and k == 0:
                                        pe.wait_ge(s_x[c], 16)
                                    for t in range(CT):
                                        w = wq_sb[:, t, k * C + g * 128:k * C + (g + 1) * 128]
                                        last = nc.tensor.matmul(slot(u), w, X[:, t, c * CH:(c + 1) * CH],
                                                                start=(t == 0), stop=(t == CT - 1))
                                    last.then_inc(s_mm, 1)
                                    if u >= 2:
                                        norms(u - 2)
                                for q in range(JT // 4):
                                    if q >= 6:
                                        pe.wait_ge(s_ve, q - 5)
                                    else:
                                        pe.wait_ge(s_ev, NU + q - 5)
                                    for r in range(4):
                                        j = 4 * q + r
                                        for t in range(CT):
                                            last = nc.tensor.matmul(
                                                slot(NU + q)[:, r * 128:(r + 1) * 128], X[:, t, j * 128:(j + 1) * 128],
                                                wq_sb[:, t, 2 * C + g * 128:2 * C + (g + 1) * 128],
                                                start=(t == 0), stop=(t == CT - 1))
                                    last.then_inc(s_vm, 1)
                                    if q < 2:
                                        norms(NU - 2 + q)
                                    if q == 3:
                                        pe.wait_ge(s_b, 2)
                                        nc.tensor.transpose(psO[0:1, 0:128], bound[:, 2:3], ident[:, :]).then_inc(s_nm, 1)

                            @block.scalar
                            def _(act):
                                for u in range(NU):
                                    k, c = divmod(u, NC)
                                    act.wait_ge(s_mm, u + 1)
                                    nc.scalar.activation(hi[k][:, c * CH:(c + 1) * CH], slot(u), ACT.Copy,
                                                         scale=QS).then_inc(s_hi, 1)
                                    if u >= 2:
                                        act.wait_ge(s_nm, u - 1)
                                    act.wait_ge(s_hi, u + 1)
                                    nc.scalar.activation(sq[u % 2][:], hi[k][:, c * CH:(c + 1) * CH], ACT.Square
                                                         ).then_inc(s_sq, 1)
                                for q in range(1, JT // 4, 2):
                                    act.wait_ge(s_vm, q + 1)
                                    act.wait_ge(s_ve, q)
                                    nc.scalar.copy(V[:, 4 * q:4 * q + 4, :].rearrange("p j n -> p (j n)"), slot(NU + q)
                                                   ).then_inc(s_ve, 1)

                            @block.vector
                            def _(dve):
                                def largest(u):
                                    dve.wait_ge(s_nm, u + 1)
                                    nc.vector.tensor_reduce(nmax[:, u:u + 1], (psO, psL)[u % 2], AX.X, ALU.max).then_inc(s_nx, 1)

                                for u in range(NU):
                                    k, c = divmod(u, NC)
                                    dve.wait_ge(s_hi, u + 1)
                                    nc.vector.scalar_tensor_tensor(
                                        out=lo[k][:, c * CH:(c + 1) * CH], in0=slot(u), scalar=QS,
                                        in1=hi[k][:, c * CH:(c + 1) * CH],
                                        op0=ALU.mult, op1=ALU.subtract).then_inc(s_ev, 1)
                                    if u >= 2:
                                        largest(u - 2)
                                largest(NU - 2)
                                largest(NU - 1)
                                dve.wait_ge(s_nx, NU)
                                nc.vector.tensor_reduce(bound[:, 0:2], nmax[:].rearrange("p (k c) -> p k c", k=2),
                                                        AX.X, ALU.max).then_inc(s_b, 1)
                                dve.wait_ge(s_b, 1)
                                nc.vector.tensor_tensor(bound[:, 2:3], bound[:, 0:1], bound[:, 1:2], ALU.mult
                                                        ).then_inc(s_b, 1)
                                dve.wait_ge(s_nm, NU + 1)
                                nc.vector.tensor_reduce(bound[0:1, 3:4], psO[0:1, 0:128], AX.X, ALU.max).then_inc(s_b, 1)
                                dve.wait_ge(s_b, 3)
                                nc.vector.tensor_scalar(safe[:], bound[0:1, 3:4], (LIMIT / SCORE) ** 2, None, ALU.is_le
                                                        ).then_inc(s_b, 1)
                                for q in range(0, JT // 4, 2):
                                    dve.wait_ge(s_vm, q + 1)
                                    if q:
                                        dve.wait_ge(s_ve, q)
                                    nc.vector.tensor_copy(V[:, 4 * q:4 * q + 4, :].rearrange("p j n -> p (j n)"), slot(NU + q)
                                                          ).then_inc(s_ve, 1)
                                dve.wait_ge(s_b, 4)

                            @block.gpsimd
                            def _(pool):
                                if g:
                                    nc.gpsimd.memset(Qst[96:97, :, :], 0.0).then_inc(s_z, 1)
                                else:
                                    nc.gpsimd.memset(Qst[96:128, :, :].bitcast(F32), 0.0).then_inc(s_z, 1)
                                    nc.gpsimd.memset(Kst[96:128, :, :].bitcast(F32), 0.0).then_inc(s_pad, 1)
                                    pool.wait_ge(s_pad, 1)
                                    nc.gpsimd.memset(Kst[96:97, :, :], MW).then_inc(s_pad, 1)
                                    pool.wait_ge(s_pad, 2)
                                pool.wait_ge(s_z, 1)

                            @block.sync
                            def _(sp):
                                if g == 0:
                                    for c in range(NC):
                                        sp.dma_start(X[:, :, c * CH:(c + 1) * CH], x_v[b, :, :, c * CH:(c + 1) * CH]
                                                     ).then_inc(s_x[c], 16)
                                n = 0
                                if g:
                                    sp.dma_start(Ls[:, g - 1, NC - 1, :], L[0:128:D, :]).then_inc(s_st, 16)
                                    n += 16
                                for k, dst, parts in ((0, Qst, (hi[0], lo[0], hi[0])), (1, Kst, (hi[1], hi[1], lo[1]))):
                                    sp.wait_ge(s_ev, NC * (k + 1))
                                    for h in range(G):
                                        for r, part in enumerate(parts):
                                            sp.dma_start(dst[r * D:(r + 1) * D, h, :],
                                                         part[h * D:(h + 1) * D, :]).then_inc(s_st, 16)
                                            n += 16
                                sp.wait_ge(s_st, n)
                        end_phase(c2, s_x + [s_pad, s_mm, s_ev, s_hi, s_st, s_sq, s_nm, s_nx, s_vm, s_ve, s_b, s_z])

                    known_safe = nc.values_load(safe[0:1, 0:1], min_val=0, max_val=1)
                    with ExitStack() as c2, nc.If(known_safe < 1):
                        mp = sb(c2, "mp", [128, G, JT, 3])
                        mcol = sb(c2, "mcol", [128, G * JT])
                        mrow = sb(c2, "mrow", [128, 128], F16)
                        s_s = sem(c2, "s_s")
                        s_m = sem(c2, "s_m")
                        s_t = sem(c2, "s_t")
                        s_r = sem(c2, "s_r")
                        parts = [(0, 3), (3, 6), (6, 8)]
                        n_it = G * len(parts)
                        with nc.Block() as block:
                            @block.gpsimd
                            def _(pool):
                                pool.sem_inc(s_m, 2)

                            @block.tensor
                            def _(pe):
                                with pe.Fori(0, JT) as it:
                                    for h in range(G):
                                        for k, (c0, c1) in enumerate(parts):
                                            o = h * 3 + k
                                            pe.wait_ge(s_m, it * n_it + o + 1)
                                            for c in range(c0, c1):
                                                last = nc.tensor.matmul(
                                                    bank[o % 2][:, (c - c0) * CH:(c - c0 + 1) * CH],
                                                    Qst[0:96, h, bass.ds(it * 128, 128)],
                                                    Kst[0:96, h, c * CH:(c + 1) * CH], start=True, stop=True)
                                            last.then_inc(s_s, 1)
                                pe.wait_ge(s_t, 1)
                                nc.tensor.transpose(psL[:, 0:128], mcol[:, :], ident[:, :]).then_inc(s_s, 1)

                            @block.vector
                            def _(dve):
                                with dve.Fori(0, JT) as it:
                                    for h in range(G):
                                        for k, (c0, c1) in enumerate(parts):
                                            o = h * 3 + k
                                            dve.wait_ge(s_s, it * n_it + o + 1)
                                            nc.vector.tensor_reduce(
                                                mp[:, h, bass.ds(it, 1), k], bank[o % 2][:, 0:(c1 - c0) * CH],
                                                AX.X, ALU.max).then_inc(s_m, 1)
                                dve.wait_ge(s_m, 2 + JT * n_it)
                                nc.vector.tensor_reduce(mcol[:, :], mp[:].rearrange("p h i k -> p (h i) k"),
                                                        AX.X, ALU.max).then_inc(s_t, 1)
                                dve.wait_ge(s_t, 1)

                            @block.scalar
                            def _(act):
                                act.wait_ge(s_s, JT * n_it + 1)
                                nc.scalar.mul(mrow[:, :], psL[:, 0:128], -1.0 / MW).then_inc(s_t, 1)

                            @block.sync
                            def _(sp):
                                sp.wait_ge(s_t, 2)
                                for h in range(G):
                                    sp.dma_start(Qst[96:97, h, :], mrow[h * JT:(h + 1) * JT, :]).then_inc(s_r, 16)
                                sp.wait_ge(s_r, 16 * G)
                        end_phase(c2, [s_s, s_m, s_t, s_r])

                    with ExitStack() as c2:
                        P = sb(c2, "P", [128, RING * G, CH])
                        acc = sb(c2, "acc", [128, 2, G, CH])
                        s_ready = sem(c2, "s_ready")
                        s_exp = sem(c2, "s_exp")
                        s_pv = sem(c2, "s_pv")
                        s_add = sem(c2, "s_add")
                        s_sum = sem(c2, "s_sum")
                        s_o_free = sem(c2, "s_o_free")
                        s_l_free = sem(c2, "s_l_free")
                        s_out = sem(c2, "s_out")
                        s_inv = sem(c2, "s_inv")
                        s_r = sem(c2, "s_ri")

                        with nc.Block() as block:
                            @block.tensor
                            def _(pe):
                                def scores(before, o, c):
                                    if before is not None:
                                        pe.wait_ge(s_exp, before)
                                    for k in range(SIZES[o]):
                                        j, h = divmod(STARTS[o] + k, G)
                                        last = nc.tensor.matmul(buf[o % NBUF][:, k * CH:(k + 1) * CH],
                                                                Kst[:, h, j * 128:(j + 1) * 128],
                                                                Qst[:, h, bass.ds(c * CH, CH)], start=True, stop=True)
                                    last.then_inc(s_ready, 1)

                                def values(c, j):
                                    pe.wait_ge(s_exp, c * NOPS + DONE_BY[j] + 1)
                                    if j == 0:
                                        pe.wait_ge(s_o_free, c + 1)
                                    for h in range(G):
                                        last = nc.tensor.matmul(psO[h * D:(h + 1) * D, :],
                                                                V[:, j, h * D:(h + 1) * D],
                                                                P[:, (j % RING) * G + h, :],
                                                                start=(j == 0), stop=(j == JT - 1))
                                    last.then_inc(s_pv, 1)

                                def row_sums(c, what, j):
                                    if (what, j) == FIRST_SUM:
                                        pe.wait_ge(s_l_free, c + 1)
                                    if what == "acc":
                                        pe.wait_ge(s_add, (c + 2) * ADDS - 1 + j)
                                    for h in range(G):
                                        src = acc[:, j, h, :] if what == "acc" else P[:, (j % RING) * G + h, :]
                                        last = nc.tensor.matmul(psL[h * D:(h + 1) * D, :], ones[:], src,
                                                                start=(what, j) == FIRST_SUM,
                                                                stop=(what, j) == LAST_SUM)
                                    last.then_inc(s_sum, 1)

                                def work(c, at):
                                    for when, what, j in WORK:
                                        if when == at:
                                            values(c, j) if what == "values" else row_sums(c, what, j)

                                def inside(c, last):
                                    for o in range(TAIL, NOPS + TAIL):
                                        if o + NBUF < NOPS:
                                            scores(c * NOPS + o + 1, o + NBUF, c)
                                        elif not last:
                                            scores(c * NOPS + o + 1, o + NBUF - NOPS, c + 1)
                                        work(c, o)
                                        if o >= NOPS and not last:
                                            work(c + 1, o - NOPS)

                                for o in range(NBUF):
                                    scores(None, o, 0)
                                for o in range(TAIL):
                                    scores(o + 1, o + NBUF, 0)
                                    work(0, o)
                                with pe.Fori(0, NC - 1) as c:
                                    inside(c, False)
                                inside(NC - 1, True)

                            @block.scalar
                            def _(act):
                                def output_out(c):
                                    act.wait_ge(s_pv, RING + (c + 1) * JT)
                                    nc.scalar.copy(O[:, g, bass.ds(c * CH, CH)], psO).then_inc(s_o_free, 1)

                                def sums_out(c):
                                    act.wait_ge(s_sum, (c + 2) * len(ORDER))
                                    act.wait_ge(s_out, 16 * (c + 1))
                                    nc.scalar.copy(L[:], psL).then_inc(s_l_free, 1)

                                def chunk(c, first):
                                    for o in range(NOPS):
                                        if o == O_AT and not first:
                                            output_out(c - 1)
                                        if o == L_AT and not first:
                                            sums_out(c - 1)
                                        act.wait_ge(s_ready, c * NOPS + o + 1)
                                        u0 = STARTS[o]
                                        j0, j1 = u0 // G, (u0 + SIZES[o] - 1) // G
                                        if j0 != j1 or u0 % G == 0:
                                            act.wait_ge(s_pv, c * JT + j1 + 1)
                                            before = (j1 - RING) % JT
                                            if before in SUM_PE:
                                                n = ORDER.index((SUMS_AT[SUM_PE.index(before)], "sums", before)) + 1
                                                act.wait_ge(s_sum, (c + (j1 >= RING)) * len(ORDER) + n)
                                            if j1 >= RING:
                                                act.wait_ge(s_add, (c + 1) * ADDS + adds_through(j1 - RING))
                                            else:
                                                act.wait_ge(s_add, c * ADDS + adds_through(j1 - RING + JT))
                                        r = u0 % (RING * G)
                                        s3 = buf[o % NBUF][:, 0:SIZES[o] * CH].rearrange("p (u n) -> p u n", n=CH)
                                        nc.scalar.activation(P[:, r:r + SIZES[o], :], s3, ACT.Exp,
                                                             scale=SCORE).then_inc(s_exp, 1)

                                chunk(0, True)
                                with act.Fori(1, NC) as c:
                                    chunk(c, False)
                                output_out(NC - 1)
                                sums_out(NC - 1)

                            @block.vector
                            def _(dve):
                                dve.sem_inc(s_pv, RING)
                                dve.sem_inc(s_add, ADDS)
                                dve.sem_inc(s_sum, len(ORDER))
                                dve.sem_inc(s_o_free, 1)
                                dve.sem_inc(s_l_free, 1)
                                dve.sem_inc(s_out, 16)

                                def chunk(c, first):
                                    for n in range(ADDS):
                                        j = SUM_V[2 * n + 1] if n < 2 else SUM_V[n + 2]
                                        dve.wait_ge(s_exp, c * NOPS + DONE_BY[j] + 1)
                                        new = P[:, (j % RING) * G:(j % RING + 1) * G, :]
                                        if n < 2:
                                            dve.wait_ge(s_sum, c * len(ORDER) + ORDER.index((ACC_AT[n], "acc", n)) + 1)
                                            j0 = SUM_V[2 * n]
                                            old = P[:, (j0 % RING) * G:(j0 % RING + 1) * G, :]
                                        else:
                                            dve.wait_ge(s_add, (c + 1) * ADDS + n - (sum_of(n) != sum_of(n - 1)))
                                            old = acc[:, sum_of(n)]
                                        nc.vector.tensor_tensor(acc[:, sum_of(n)], old, new, ALU.add).then_inc(s_add, 1)
                                        if n == ADDS // 2 and not first:
                                            dve.wait_ge(s_out, 16 * (c + 1))
                                            nc.vector.reciprocal(Ls[:, g, bass.ds(c - 1, 1), :],
                                                                 Ls[:, g, bass.ds(c - 1, 1), :]).then_inc(s_inv, 1)

                                chunk(0, True)
                                with dve.Fori(1, NC) as c:
                                    chunk(c, False)

                            @block.sync
                            def _(sp):
                                with sp.Fori(0, NC - 1) as c:
                                    sp.wait_ge(s_l_free, c + 2)
                                    sp.dma_start(Ls[:, g, bass.ds(c, 1), :], L[0:128:D, :]).then_inc(s_out, 16)
                                    sp.wait_ge(s_inv, c + 1)
                                    sp.dma_start(r_dram[b, g * G:(g + 1) * G, bass.ds(c * CH, CH)],
                                                 Ls[:, g, bass.ds(c, 1), :]).then_inc(s_r, 16)
                                sp.wait_ge(s_l_free, NC + 1)
                                sp.wait_ge(s_r, 16 * (NC - 1))
                        end_phase(c2, [s_ready, s_exp, s_pv, s_add, s_sum, s_o_free, s_l_free, s_out, s_inv, s_r])

        def layer1(b):
            with ExitStack() as ctx:
                ww_sb = sb(ctx, "ww_sb", [128, CT, C])
                s_ww = sem(ctx, "s_ww")
                Yh = sb(ctx, "Yh", [128, CT, N], F16)
                Yl = sb(ctx, "Yl", [128, CT, N], F16)
                s_yh = sem(ctx, "s_yh")
                s_yl = sem(ctx, "s_yl")
                s_rec = sem(ctx, "s_rec")
                s_mm = sem(ctx, "s_mm1")
                s_ev = sem(ctx, "s_ev1")
                with ExitStack() as c2:
                    R = sb(c2, "R", [128, CT, N])
                    s_l = sem(c2, "s_l")
                    s_norm = sem(c2, "s_norm")
                    s_rc = [sem(c2, f"s_rc{c}") for c in range(NC)]
                    with nc.Block() as block:
                        @block.sync
                        def _(sp):
                            def spread(c):
                                cs = slice(c * CH, (c + 1) * CH)
                                for g in range(NG):
                                    sp.dma_start(R[:, g, cs], r_dram[b, g * G:(g + 1) * G, cs].unsqueeze(1)
                                                 .broadcast_to([G, D, CH])).then_inc(s_rc[c], 16)

                            sp.dma_start(Ls[:, NG - 1, NC - 1, :], L[0:128:D, :]).then_inc(s_l, 16)
                            for c in range(4):
                                spread(c)
                            sp.wait_ge(s_rec, 1)
                            for g in range(NG):
                                sp.dma_start(r_dram[b, g * G:(g + 1) * G, N - CH:N], Ls[:, g, NC - 1, :]
                                             ).then_inc(s_l, 16)
                            for c in range(4, NC - 1):
                                spread(c)
                            sp.wait_ge(s_l, 16 * NG + 16)
                            spread(NC - 1)
                            sp.dma_start(ww_sb[:], ww.rearrange("(t p) o -> p t o", p=128)).then_inc(s_ww, 16)
                            sp.wait_ge(s_ww, 16)

                        @block.vector
                        def _(dve):
                            def normalise(c):
                                cs = slice(c * CH, (c + 1) * CH)
                                dve.wait_ge(s_rc[c], 16 * NG)
                                nc.vector.tensor_tensor(O[:, :, cs], O[:, :, cs], R[:, :, cs], ALU.mult
                                                        ).then_inc(s_norm, 1)

                            def low(u):
                                c, t = divmod(u, CT)
                                cs = slice(c * CH, (c + 1) * CH)
                                dve.wait_ge(s_yh, u + 1)
                                nc.vector.scalar_tensor_tensor(out=Yl[:, t, cs], in0=X[:, t, cs], scalar=QS,
                                                               in1=Yh[:, t, cs], op0=ALU.mult, op1=ALU.subtract
                                                               ).then_inc(s_yl, 1)

                            normalise(0)
                            dve.wait_ge(s_l, 16)
                            nc.vector.reciprocal(Ls[:, :, NC - 1, :], Ls[:, :, NC - 1, :]).then_inc(s_rec, 1)
                            for u in range(NC * CT):
                                c, t = divmod(u, CT)
                                if t == 0 and c + 1 < NC:
                                    normalise(c + 1)
                                cs = slice(c * CH, (c + 1) * CH)
                                dve.wait_ge(s_mm, u + 1)
                                nc.vector.tensor_tensor(X[:, t, cs], X[:, t, cs], slot(u), ALU.add
                                                        ).then_inc(s_ev, 1)
                                if u:
                                    low(u - 1)
                            low(NC * CT - 1)
                            dve.wait_ge(s_yl, NC * CT)

                        @block.scalar
                        def _(act):
                            for u in range(NC * CT):
                                c, t = divmod(u, CT)
                                act.wait_ge(s_ev, u + 1)
                                nc.scalar.activation(Yh[:, t, c * CH:(c + 1) * CH], X[:, t, c * CH:(c + 1) * CH],
                                                     ACT.Copy, scale=QS).then_inc(s_yh, 1)

                        @block.tensor
                        def _(pe):
                            for u in range(NC * CT):
                                c, t = divmod(u, CT)
                                pe.wait_ge(s_norm, c + 1)
                                if u >= 6:
                                    pe.wait_ge(s_ev, u - 5)
                                for k in range(CT):
                                    last = nc.tensor.matmul(slot(u), wp_sb[:, k, t * 128:(t + 1) * 128],
                                                            O[:, k, c * CH:(c + 1) * CH],
                                                            start=(k == 0), stop=(k == CT - 1))
                                last.then_inc(s_mm, 1)
                    end_phase(c2, [s_rec, s_ww, s_yh, s_yl, s_mm, s_ev, s_l, s_norm] + s_rc)

                TA = sb(ctx, "TA", [128, N], F16)
                TB = sb(ctx, "TB", [128, N], F16)
                PA = sb(ctx, "PA", [128, M], F16)
                PB = sb(ctx, "PB", [128, M], F16)
                GTh = sb(ctx, "GTh", [128, MT, C], F16)
                GTl = sb(ctx, "GTl", [128, MT, C], F16)
                s_pad = sem(ctx, "s_pad1")
                with ExitStack() as c2:
                    th = sb(c2, "th", [CM, 2, CH])
                    ph = sb(c2, "ph", [CM, M])
                    Gp = sb(c2, "Gp", [128, CT, M])
                    pooled = sb(c2, "pooled", [128, 2, CH // 4])
                    s_pool = sem(c2, "s_pool")
                    s_hi = sem(c2, "s_hi1")
                    s_lo = sem(c2, "s_lo1")
                    s_gh = sem(c2, "s_gh")
                    s_cp = sem(c2, "s_cp")
                    UN = 4
                    with nc.Block() as block:
                        @block.gpsimd
                        def _(pool):
                            nc.gpsimd.memset(TB[CM:128, :].bitcast(F32), 0.0).then_inc(s_pad, 1)
                            nc.gpsimd.memset(PB[CM:128, :].bitcast(F32), 0.0).then_inc(s_pad, 1)
                            pool.wait_ge(s_pad, 2)
                            nc.gpsimd.memset(PB[CM:CM + 1, :], MW1).then_inc(s_pad, 1)
                            pool.wait_ge(s_pad, 3)

                        @block.tensor
                        def _(pe):
                            for u in range(UN * NC):
                                c, k = divmod(u, UN)
                                cs = slice(c * CH, (c + 1) * CH)
                                if u >= 6:
                                    pe.wait_ge(s_ev, u - 5)
                                o0, o1 = ((0, CM), (CM, 2 * CM), (2 * CM, 2 * CM + 128), (2 * CM + 128, 2 * CM + C))[k]
                                terms = [(w[:, t, o0:o1], y[:, t, cs]) for t in range(CT if k else 1)
                                         for w, y in ((cw[0], Yh), (cw[1], Yh), (cw[0], Yl))]
                                for n, (w, y) in enumerate(terms):
                                    last = nc.tensor.matmul(slot(u)[0:o1 - o0, :], w, y,
                                                            start=(n == 0), stop=(n == len(terms) - 1))
                                last.then_inc(s_mm, 1)
                            for m in range(MT):
                                pe.wait_ge(s_ev, max(UN * NC + m - 5, UN * (m * 128 * NC // M + 1)))
                                for t in range(CT):
                                    last = nc.tensor.matmul(slot(UN * NC + m)[:, 0:C], Gp[:, t, m * 128:(m + 1) * 128],
                                                            ww_sb[:, t, :], start=(t == 0), stop=(t == CT - 1))
                                last.then_inc(s_mm, 1)

                        @block.scalar
                        def _(act):
                            for c in range(NC):
                                act.wait_ge(s_ev, UN * c + 1)
                                nc.scalar.activation(TA[0:CM, c * CH:(c + 1) * CH], th[:, c % 2, :], ACT.Copy,
                                                     scale=QS).then_inc(s_hi, 1)
                            act.wait_ge(s_ev, UN * NC)
                            nc.scalar.activation(PA[0:CM, :], ph[:], ACT.Copy, scale=QS).then_inc(s_hi, 1)
                            for m in range(MT):
                                act.wait_ge(s_mm, UN * NC + m + 1)
                                nc.scalar.activation(GTh[:, m, :], slot(UN * NC + m)[:, 0:C], ACT.Copy, scale=QS).then_inc(s_gh, 1)

                        @block.vector
                        def _(dve):
                            pools = 0
                            for u in range(UN * NC):
                                c, k = divmod(u, UN)
                                cs = slice(c * CH, (c + 1) * CH)
                                dve.wait_ge(s_mm, u + 1)
                                if k == 0:
                                    nc.vector.tensor_scalar(th[:, c % 2, :], slot(u)[0:CM, :],
                                                            YS, tb_sb[:, 0:1], ALU.mult, ALU.add).then_inc(s_ev, 1)
                                    continue
                                P0 = CM if k == 1 else 128
                                q = CH // 4
                                tmp = pooled[0:P0, pools % 2, :]
                                src = slot(u)[0:P0, :].rearrange("p (a u b v) -> p a b u v", u=2, v=2, b=W // 2)
                                nc.vector.tensor_reduce(tmp.rearrange("p (a b) -> p a b", b=W // 2), src, AX.XY,
                                                        ALU.max).then_inc(s_pool, 1)
                                pools += 1
                                dve.wait_ge(s_pool, pools)
                                dst = ph[:, c * q:(c + 1) * q] if k == 1 else Gp[:, k - 2, c * q:(c + 1) * q]
                                bias = tb_sb[:, 1:2] if k == 1 else col[:, k - 2, 0:1]
                                nc.vector.tensor_scalar(dst, tmp, YS, bias, ALU.mult, ALU.add).then_inc(s_ev, 1)
                                if k == 1:
                                    dve.wait_ge(s_hi, c + 1)
                                    nc.vector.scalar_tensor_tensor(
                                        out=TA[CM:128, cs], in0=th[:, c % 2, :], scalar=QS, in1=TA[0:CM, cs],
                                        op0=ALU.mult, op1=ALU.subtract).then_inc(s_lo, 1)
                            dve.wait_ge(s_hi, NC + 1)
                            nc.vector.scalar_tensor_tensor(out=PB[0:CM, :], in0=ph[:], scalar=QS, in1=PA[0:CM, :],
                                                           op0=ALU.mult, op1=ALU.subtract).then_inc(s_lo, 1)
                            for m in range(MT):
                                dve.wait_ge(s_gh, m + 1)
                                nc.vector.scalar_tensor_tensor(out=GTl[:, m, :], in0=slot(UN * NC + m)[:, 0:C], scalar=QS,
                                                               in1=GTh[:, m, :], op0=ALU.mult, op1=ALU.subtract
                                                               ).then_inc(s_ev, 1)
                            dve.wait_ge(s_lo, NC + 1)
                            dve.wait_ge(s_ev, UN * NC + MT)

                        @block.sync
                        def _(sp):
                            sp.wait_ge(s_hi, NC)
                            sp.dma_start(TB[0:CM, :], TA[0:CM, :]).then_inc(s_cp, 16)
                            sp.wait_ge(s_hi, NC + 1)
                            sp.dma_start(PA[CM:128, :], PA[0:CM, :]).then_inc(s_cp, 16)
                            sp.wait_ge(s_cp, 32)
                    end_phase(c2, [s_pad, s_pool, s_mm, s_ev, s_hi, s_lo, s_gh, s_cp])

                with ExitStack() as c2:
                    R1 = sb(c2, "R1", [128, N])
                    mx = sb(c2, "mx", [128, JT])
                    m16 = sb(c2, "m16", [128, JT], F16)
                    l1 = sb(c2, "l1", [128, JT])
                    stat = sb(c2, "stat", [128, 2, JT])
                    sumT = sb(c2, "sumT", [JT, 128])
                    m16T = sb(c2, "m16T", [JT // 2, 2, 128], F16)
                    junk = sb(c2, "junk", [128, 2, M])
                    P32 = O[:].rearrange("p t (m n) -> p t m n", n=CH)
                    Ph = sb(c2, "Ph", [128, 2, MT, CH], F16)
                    Pl = sb(c2, "Pl", [128, 2, MT, CH], F16)
                    z = sb(c2, "z", [128, 2, CH])
                    res = sb(c2, "res", [128, 2, CH])
                    s_s0 = sem(c2, "s_s0")
                    s_mx = sem(c2, "s_mx")
                    s_m16 = sem(c2, "s_m16")
                    s_mb = sem(c2, "s_mb")
                    s_e0 = sem(c2, "s_e0")
                    s_n = sem(c2, "s_n")
                    s_tr = sem(c2, "s_tr")
                    s_t = sem(c2, "s_t1")
                    s_row = sem(c2, "s_row")
                    s_r1 = sem(c2, "s_r1")
                    s_s = sem(c2, "s_s1")
                    s_e = sem(c2, "s_e1")
                    s_h = sem(c2, "s_h1")
                    s_l = sem(c2, "s_l1")
                    s_y = sem(c2, "s_y")
                    s_yf = sem(c2, "s_yf")
                    s_res = sem(c2, "s_res")
                    s_st = sem(c2, "s_st1")
                    SZ = [3, 3, 2]
                    NE = len(SZ)
                    buf4 = buf + [psOL[:, :]]
                    HALF = JT // 2
                    TURN = HALF + 2
                    with nc.Block() as block:
                        @block.gpsimd
                        def _(pool):
                            for i in range(JT):
                                pool.wait_ge(s_mx, i + 1)
                                nc.gpsimd.tensor_scalar(m16[:, i:i + 1], mx[:, i:i + 1], -SCORE1, None, ALU.mult
                                                        ).then_inc(s_m16, 1)
                                pool.wait_ge(s_m16, i + 1)
                                nc.gpsimd.tensor_copy(stat[:, 0, i:i + 1], m16[:, i:i + 1]).then_inc(s_mb, 1)

                        @block.tensor
                        def _(pe):
                            for i in range(JT):
                                if i >= 4:
                                    pe.wait_ge(s_e0, i - 3)
                                if i == TURN:
                                    pe.wait_ge(s_mb, HALF)
                                    nc.tensor.transpose(buf4[i % 4][0:HALF, 0:128], stat[:, 0, 0:HALF],
                                                        ident[:, :]).then_inc(s_tr, 1)
                                    pe.wait_ge(s_t, 1)
                                its = slice(i * 128, (i + 1) * 128)
                                for k in range(M // CH):
                                    ks = slice(k * CH, (k + 1) * CH)
                                    nc.tensor.matmul(buf4[i % 4][:, ks], TA[:, its], PA[:, ks], start=True, stop=False)
                                    last = nc.tensor.matmul(buf4[i % 4][:, ks], TB[:, its], PB[:, ks],
                                                            start=False, stop=True)
                                last.then_inc(s_s0, 1)

                            def scores(c, p, k):
                                o = NE * p + k
                                for r in range(SZ[k]):
                                    m = slice((3 * k + r) * 128, (3 * k + r + 1) * 128)
                                    dst = bank[o % 2][:, r * CH:(r + 1) * CH]
                                    nc.tensor.matmul(dst, PA[:, m], TA[:, bass.ds(c * CH, CH)], start=True, stop=False)
                                    last = nc.tensor.matmul(dst, PB[:, m], TB[:, bass.ds(c * CH, CH)],
                                                            start=False, stop=True)
                                last.then_inc(s_s, 1)

                            def output(c, p, t):
                                pe.wait_ge(s_yf, c * 2 + t + 1)
                                ts = slice(t * 128, (t + 1) * 128)
                                n = 0
                                for k in range(NE):
                                    pe.wait_ge(s_l, (c + 2) * NE + k + 1)
                                    for m in range(3 * k, 3 * k + SZ[k]):
                                        for w, v in ((GTh, Ph), (GTl, Ph), (GTh, Pl)):
                                            last = nc.tensor.matmul(psOL[:, t * CH:(t + 1) * CH], w[:, m, ts],
                                                                    v[:, p, m, :], start=(n == 0), stop=(n == 3 * MT - 1))
                                            n += 1
                                last.then_inc(s_y, 1)

                            def step(c, p, go_on):
                                for k in range(NE):
                                    if go_on:
                                        pe.wait_ge(s_e, c * NE + k + 2)
                                        scores(c + 1, 1 - p, k)
                                    if k >= 1:
                                        output(c, p, k - 1)

                            pe.wait_ge(s_row, 16)
                            for k in range(2):
                                pe.wait_ge(s_e0, JT - 2 + k)
                                scores(0, 0, k)
                            pe.wait_ge(s_e0, JT)
                            pe.wait_ge(s_mb, JT)
                            nc.tensor.transpose(psL[0:HALF, 0:128], stat[:, 0, HALF:JT], ident[:, :]).then_inc(s_tr, 1)
                            pe.wait_ge(s_n, 1)
                            nc.tensor.transpose(psO[0:JT, 0:128], stat[:, 1, :], ident[:, :]).then_inc(s_tr, 1)
                            pe.wait_ge(s_e, 1)
                            scores(0, 0, 2)
                            pe.wait_ge(s_t, 3)
                            step(0, 0, True)
                            pe.wait_ge(s_row, 32)
                            with pe.Fori(0, NC // 2 - 1) as i:
                                step(2 * i + 1, 1, True)
                                step(2 * i + 2, 0, True)
                            step(NC - 1, 1, False)

                        @block.scalar
                        def _(act):
                            for i in range(JT):
                                if i == TURN - 2:
                                    act.wait_ge(s_tr, 1)
                                    nc.scalar.copy(m16T[:, 0, :], buf4[TURN % 4][0:HALF, 0:128]).then_inc(s_t, 1)
                                act.wait_ge(s_mb, i + 1)
                                if i >= 2:
                                    act.wait_ge(s_e0, i - 1)
                                nc.scalar.activation(junk[:, i % 2, :], buf4[i % 4], ACT.Exp, bias=stat[:, 0, i:i + 1],
                                                     scale=SCORE1, accum_out=l1[:, i:i + 1]).then_inc(s_e0, 1)

                            def exps(c, p):
                                for k in range(NE):
                                    o = NE * p + k
                                    ms = slice(3 * k, 3 * k + SZ[k])
                                    act.wait_ge(s_s, c * NE + k + 1)
                                    act.wait_ge(s_l, c * NE + k + 1)
                                    nc.scalar.activation(
                                        P32[:, p, ms, :],
                                        bank[o % 2][:, 0:SZ[k] * CH].rearrange("p (u n) -> p u n", n=CH),
                                        ACT.Exp, scale=SCORE1).then_inc(s_e, 1)
                                    act.wait_ge(s_e, c * NE + k + 1)
                                    if k == 0:
                                        act.wait_ge(s_y, c * 2 + 2)
                                    nc.scalar.activation(Ph[:, p, ms, :], P32[:, p, ms, :], ACT.Copy, scale=PS
                                                         ).then_inc(s_h, 1)

                            with act.Fori(0, NC // 2) as i:
                                exps(2 * i, 0)
                                exps(2 * i + 1, 1)

                        @block.vector
                        def _(dve):
                            dve.sem_inc(s_l, 2 * NE)
                            dve.sem_inc(s_y, 4)
                            dve.sem_inc(s_yf, 2)
                            dve.sem_inc(s_st, 16)
                            for i in range(JT):
                                dve.wait_ge(s_s0, i + 1)
                                nc.vector.tensor_reduce(mx[:, i:i + 1], buf4[i % 4], AX.X, ALU.max).then_inc(s_mx, 1)
                            dve.wait_ge(s_e0, JT)
                            nc.vector.reciprocal(stat[:, 1, :], l1[:]).then_inc(s_n, 1)
                            dve.wait_ge(s_tr, 2)
                            nc.vector.tensor_copy(m16T[:, 1, :], psL[0:HALF, 0:128]).then_inc(s_t, 1)
                            dve.wait_ge(s_tr, 3)
                            nc.vector.tensor_copy(sumT[:], psO[0:JT, 0:128]).then_inc(s_t, 1)

                            def lows(c, p):
                                for k in range(NE):
                                    ms = slice(3 * k, 3 * k + SZ[k])
                                    dve.wait_ge(s_h, c * NE + k + 1)
                                    nc.vector.scalar_tensor_tensor(
                                        out=Pl[:, p, ms, :], in0=P32[:, p, ms, :], scalar=PS, in1=Ph[:, p, ms, :],
                                        op0=ALU.mult, op1=ALU.subtract).then_inc(s_l, 1)

                            def results(c):
                                ns = bass.ds(c * CH, CH)
                                for t in range(CT):
                                    dve.wait_ge(s_y, c * 2 + t + 5)
                                    nc.vector.scalar_tensor_tensor(
                                        out=z[:, t, :], in0=psOL[:, t * CH:(t + 1) * CH], scalar=sA[:, t, 3:4],
                                        in1=R1[:, ns], op0=ALU.mult, op1=ALU.mult).then_inc(s_yf, 1)
                                    dve.wait_ge(s_yf, c * 2 + t + 3)
                                    dve.wait_ge(s_st, c * 32 + 16 * (t + 1))
                                    nc.vector.scalar_tensor_tensor(
                                        out=res[:, t, :], in0=z[:, t, :], scalar=sA[:, t, 2:3],
                                        in1=X[:, t, ns], op0=ALU.add, op1=ALU.add).then_inc(s_res, 1)

                            lows(0, 0)
                            dve.wait_ge(s_r1, 32)
                            lows(1, 1)
                            results(0)
                            with dve.Fori(0, NC // 2 - 1) as i:
                                lows(2 * i + 2, 0)
                                results(2 * i + 1)
                                lows(2 * i + 3, 1)
                                results(2 * i + 2)
                            results(NC - 1)

                        @block.sync
                        def _(sp):
                            for k in range(2):
                                sp.wait_ge(s_t, k + 1)
                                sp.dma_start(TB[CM:CM + 1, k * N // 2:(k + 1) * N // 2], m16T[:, k, :]
                                             ).then_inc(s_row, 16)
                            sp.wait_ge(s_t, 3)
                            sp.dma_start(r1_dram[b, 0:1, :].rearrange("a (i n) -> (a i) n", n=128), sumT[:]
                                         ).then_inc(s_r1, 16)
                            sp.wait_ge(s_r1, 16)
                            sp.dma_start(R1[:], r1_dram[b, 0:1, :].broadcast_to([128, N])).then_inc(s_r1, 16)
                            sp.wait_ge(s_row, 32)
                            with sp.Fori(0, NC) as c:
                                for t in range(CT):
                                    sp.wait_ge(s_res, c * 2 + t + 1)
                                    sp.dma_start(out_v[b, :, t, bass.ds(c * CH, CH)], res[:, t, :]).then_inc(s_st, 16)
                            sp.wait_ge(s_st, 16 * (CT * NC + 1))
                    end_phase(c2, [s_s0, s_mx, s_m16, s_mb, s_e0, s_n, s_tr, s_t, s_row, s_r1, s_s, s_e, s_h, s_l, s_y, s_yf,
                                   s_res, s_st])

        with nc.Fori(0, B) as b:
            layer0(b)
            layer1(b)


def kernel(**inputs):
    import numpy as _np
    import concourse.bacc as _bacc
    from concourse import mybir as _mybir
    from concourse.bass_utils import run_bass_kernel_spmd as _run

    def stacked(*names):
        return _np.stack([_np.asarray(inputs[f"L1_conv_{name}"]) for name in names], axis=1)

    weights = [_np.asarray(inputs[name]).T for name in (
        "L0_conv_w_qkv", "L0_conv_w_proj", "L1_conv_g_w", "L1_conv_theta_w", "L1_conv_phi_w", "L1_conv_W_w")]
    laid_out = [_np.asarray(inputs["x"]).reshape(B, C, N)] + weights + [
        stacked("g_b", "W_b", "bn_gamma", "bn_beta", "bn_mean", "bn_var"), stacked("theta_b", "phi_b")]
    nc = _bacc.Bacc("TRN2", target_bir_lowering=False, num_devices=1)
    arrays, args = {}, []
    for name, a in zip(("x", "w_qkv", "w_proj", "g_w", "theta_w", "phi_w", "W_w", "vectors", "biases"), laid_out):
        a = _np.ascontiguousarray(a)
        arrays[f"in_{name}"] = a
        args.append(nc.dram_tensor(f"in_{name}", a.shape, _mybir.dt.from_np(a.dtype), kind="ExternalInput").ap())
    args.append(nc.dram_tensor("out", (B, C, N), _mybir.dt.float32, kind="ExternalOutput").ap())
    args.append(nc.dram_tensor("att_inv", (B, HEADS, N), _mybir.dt.float32, kind="Internal").ap())
    args.append(nc.dram_tensor("pool_inv", (B, 1, N), _mybir.dt.float32, kind="Internal").ap())
    conv_seq(nc, *args)
    r = _run(nc, [arrays], core_ids=[0])
    return r.results[0]["out"].reshape(B, C, H, W)
```
